# Optimizing a Trainium2 kernel written in Bass

```python
import numpy as np
import jax
import jax.numpy as jnp

def _softmax(x, axis=-1):
    return jax.nn.softmax(x, axis=axis)

def _gelu(x):
    return jax.nn.gelu(x, approximate=True)

def _silu(x):
    return jax.nn.silu(x)

def _sigmoid(x):
    return jax.nn.sigmoid(x)

def _layernorm(x, axis=-1, eps=1e-05):
    m = jnp.mean(x, axis=axis, keepdims=True)
    v = jnp.var(x, axis=axis, keepdims=True)
    return (x - m) / jnp.sqrt(v + eps)

def _scatter_add(tgt, idx, src, axis=0):
    return tgt.at[idx].add(src)

def _segment_sum(src, seg, n):
    return jax.ops.segment_sum(src, seg, n)
kernel_name = 'mk_adaln_d1_jaxref_r8_c0910b'

def setup_inputs(seed: int=0):
    np.random.seed(seed)
    _w = jnp.asarray

    def _L0_attn_setup():
        import jax, jax.numpy as jnp
        import numpy as np
        NUM_HEADS = 16
        BASE = 10000.0

        def _rope(t, cos_t, sin_t):
            k_max = t.shape[-1] // 2
            tr = t.reshape(*t.shape[:-1], k_max, 2)
            x0, x1 = (tr[..., 0], tr[..., 1])
            out = jnp.stack([cos_t * x0 - sin_t * x1, sin_t * x0 + cos_t * x1], axis=-1)
            return out.reshape(t.shape)
        key = jax.random.key(seed)
        ks = jax.random.split(key, 5)
        b, n, c = (4, 512, 128)
        return {'x': jax.random.normal(ks[0], (b, n, c), jnp.float32), 'W_qk': jax.random.normal(ks[1], (2 * c, c), jnp.float32) * 0.02, 'b_qk': jax.random.normal(ks[2], (2 * c,), jnp.float32) * 0.02, 'lepe_w': jax.random.normal(ks[3], (c, 1, 3), jnp.float32) * 0.1, 'lepe_b': jax.random.normal(ks[4], (c,), jnp.float32) * 0.02}
    _L0_attn_in = _L0_attn_setup()

    def _L0_ffn_setup():
        import jax, jax.numpy as jnp
        import numpy as np
        B, N, DIM = (2, 256, 128)
        HEADS, DIM_HEAD, EXPERTS = (8, 64, 8)
        SCALE = DIM_HEAD ** (-0.5)
        key = jax.random.key(seed)
        ks = jax.random.split(key, 6)
        dim_inner = HEADS * DIM_HEAD
        return {'x': jax.random.normal(ks[0], (B, N, DIM), jnp.float32), 'w_q': jax.random.normal(ks[1], (DIM, dim_inner), jnp.float32) * 0.02, 'w_k': jax.random.normal(ks[2], (DIM, dim_inner), jnp.float32) * 0.02, 'w_gate': jax.random.normal(ks[3], (DIM, HEADS * EXPERTS), jnp.float32) * 0.02, 'value_experts': jax.random.normal(ks[4], (EXPERTS, HEADS, DIM, DIM_HEAD), jnp.float32) * 0.02, 'output_experts': jax.random.normal(ks[5], (EXPERTS, HEADS, DIM_HEAD, DIM), jnp.float32) * 0.02}
    _L0_ffn_in = _L0_ffn_setup()
    _L0_c = _w((lambda *s: np.random.randn(*s).astype(np.float32) * 0.05)(4, 128))
    _L0_wmod = _w((lambda *s: np.random.randn(*s).astype(np.float32) * 0.05)(128, 6 * 128) * 128 ** (-0.5))
    _d = {'L0_attn_x': _L0_attn_in['x'], 'L0_attn_W_qk': _L0_attn_in['W_qk'], 'L0_attn_b_qk': _L0_attn_in['b_qk'], 'L0_attn_lepe_w': _L0_attn_in['lepe_w'], 'L0_attn_lepe_b': _L0_attn_in['lepe_b'], 'L0_ffn_w_q': _L0_ffn_in['w_q'], 'L0_ffn_w_k': _L0_ffn_in['w_k'], 'L0_ffn_w_gate': _L0_ffn_in['w_gate'], 'L0_ffn_value_experts': _L0_ffn_in['value_experts'], 'L0_ffn_output_experts': _L0_ffn_in['output_experts'], 'L0_c': _L0_c, 'L0_wmod': _L0_wmod}
    _x0 = _d['L0_attn_x']
    _d['L0_attn_x'] = jax.random.normal(jax.random.fold_in(jax.random.key(seed), 1), (4, 1024, 128), dtype=_x0.dtype)
    del _x0
    return _d

def reference(L0_attn_x, L0_attn_W_qk, L0_attn_b_qk, L0_attn_lepe_w, L0_attn_lepe_b, L0_ffn_w_q, L0_ffn_w_k, L0_ffn_w_gate, L0_ffn_value_experts, L0_ffn_output_experts, L0_c, L0_wmod):

    def _L0_attn_ref(x, W_qk, b_qk, lepe_w, lepe_b):
        import jax, jax.numpy as jnp
        import numpy as np
        NUM_HEADS = 16
        BASE = 10000.0

        def _rope(t, cos_t, sin_t):
            k_max = t.shape[-1] // 2
            tr = t.reshape(*t.shape[:-1], k_max, 2)
            x0, x1 = (tr[..., 0], tr[..., 1])
            out = jnp.stack([cos_t * x0 - sin_t * x1, sin_t * x0 + cos_t * x1], axis=-1)
            return out.reshape(t.shape)
        b, n, c = x.shape
        h = NUM_HEADS
        d = c // h
        k_max = c // 2
        theta = 1.0 / BASE ** (jnp.arange(k_max, dtype=jnp.float32) / k_max)
        cos_t, sin_t = (jnp.cos(theta), jnp.sin(theta))
        qk = x @ W_qk.T + b_qk
        q = jax.nn.elu(qk[..., :c]) + 1.0
        k = jax.nn.elu(qk[..., c:]) + 1.0
        q_rope = _rope(q, cos_t, sin_t).reshape(b, n, h, d).transpose(0, 2, 1, 3)
        k_rope = _rope(k, cos_t, sin_t).reshape(b, n, h, d).transpose(0, 2, 1, 3)
        qh = q.reshape(b, n, h, d).transpose(0, 2, 1, 3)
        kh = k.reshape(b, n, h, d).transpose(0, 2, 1, 3)
        vh = x.reshape(b, n, h, d).transpose(0, 2, 1, 3)
        z = 1.0 / (jnp.einsum('bhnd,bhd->bhn', qh, kh.mean(axis=2)) + 1e-06)
        kv = jnp.einsum('bhnd,bhne->bhde', k_rope, vh) * (1.0 / n)
        attn = jnp.einsum('bhnd,bhde->bhne', q_rope, kv) * z[..., None]
        out = attn.transpose(0, 2, 1, 3).reshape(b, n, c)
        v_cn = x.transpose(0, 2, 1)
        pe = jax.lax.conv_general_dilated(v_cn, lepe_w, window_strides=(1,), padding=((1, 1),), feature_group_count=c, dimension_numbers=('NCH', 'OIH', 'NCH'))
        pe = pe + lepe_b[None, :, None]
        return out + pe.transpose(0, 2, 1)

    def _L0_ffn_ref(x, w_q, w_k, w_gate, value_experts, output_experts):
        import jax, jax.numpy as jnp
        import numpy as np
        B, N, DIM = (2, 256, 128)
        HEADS, DIM_HEAD, EXPERTS = (8, 64, 8)
        SCALE = DIM_HEAD ** (-0.5)
        b, n, _ = x.shape
        q = (x @ w_q).reshape(b, n, HEADS, DIM_HEAD).transpose(0, 2, 1, 3)
        k = (x @ w_k).reshape(b, n, HEADS, DIM_HEAD).transpose(0, 2, 1, 3)
        gates = jax.nn.sigmoid((x @ w_gate).reshape(b, n, HEADS, EXPERTS).transpose(0, 2, 1, 3))
        sel = jnp.argmax(gates, axis=-1)
        gm = jax.nn.one_hot(sel, EXPERTS, dtype=x.dtype) * gates
        values = jnp.einsum('bhne,ehdk,bnd->bhnk', gm, value_experts, x)
        sim = jnp.einsum('bhid,bhjd->bhij', q * SCALE, k)
        causal_mask = jnp.triu(jnp.ones((n, n), dtype=bool), 1)
        sim = jnp.where(causal_mask, jnp.finfo(sim.dtype).min, sim)
        attn = jax.nn.softmax(sim, axis=-1)
        out = jnp.einsum('bhij,bhjk->bhik', attn, values)
        out = jnp.einsum('bhne,ehkd,bhnk->bhnd', gm, output_experts, out)
        return out.sum(axis=1)
    x = L0_attn_x
    mod = (_silu(L0_c) @ L0_wmod).reshape(L0_c.shape[0], 6, 1, -1)
    sa, ca, ga, sb, cb, gb = (mod[:, 0], mod[:, 1], mod[:, 2], mod[:, 3], mod[:, 4], mod[:, 5])
    ga = (2 * (ga >= 0) - 1) * jnp.maximum(jnp.abs(ga), 0.25)
    gb = (2 * (gb >= 0) - 1) * jnp.maximum(jnp.abs(gb), 0.25)
    h = _layernorm(x, axis=-1) * (1 + ca) + sa
    x = x + ga * _L0_attn_ref(h, L0_attn_W_qk, L0_attn_b_qk, L0_attn_lepe_w, L0_attn_lepe_b)
    h = _layernorm(x, axis=-1) * (1 + cb) + sb
    x = x + gb * _L0_ffn_ref(h, L0_ffn_w_q, L0_ffn_w_k, L0_ffn_w_gate, L0_ffn_value_experts, L0_ffn_output_experts)
    return x

_drawn_inputs = setup_inputs


def setup_inputs(seed=0):
    import zlib

    import numpy as np

    out = dict(_drawn_inputs(seed))
    spreads = {}
    factors = {'L0_attn_W_qk': 8.0,
     'L0_attn_b_qk': 24.395,
     'L0_attn_lepe_b': 8.0,
     'L0_ffn_w_q': 8.0,
     'L0_ffn_w_k': 8.0,
     'L0_ffn_w_gate': 8.0,
     'L0_ffn_value_experts': 8.0,
     'L0_ffn_output_experts': 8.0}
    for name, (base, spread) in spreads.items():
        noise = np.random.default_rng([zlib.crc32(name.encode()), seed]).standard_normal(out[name].shape)
        drawn = base * np.exp(spread * noise) if base else spread * noise
        out[name] = jnp.asarray(drawn.astype(out[name].dtype))
    for name, factor in factors.items():
        out[name] = (out[name] * factor).astype(out[name].dtype)
    return out
```

```python
from contextlib import ExitStack

import numpy as np

import concourse.bass as bass
from concourse import mybir

B, N, C = 4, 1024, 128
T = N // 128
LH = 16
LD = C // LH
H, K, E = 8, 64, 8
HP = H // 2
EC = E * K // 128
SCALE = float(K) ** -0.5
EPS = 1e-5
MASKED = -1e30
SATURATED = 17.0
MOD_SA, MOD_CA, MOD_GA, MOD_SB, MOD_CB, MOD_GB = range(6)

CONSTS = {"ident": C, "rot": C, "rot_t": C, "same_head": C, "head_of": LH, "rank": E, "expert_of": EC,
          "causal": 128, "causal_t": 128, "row_of": H * 128}
KEPT = 7
CONST_AT = {n: sum(list(CONSTS.values())[:i]) for i, n in enumerate(CONSTS)}

MAX_ORDER = [4, 0, 5, 1, 6, 2, 7, 3]
KEY_ORDER = [0, 4, 1, 5, 2, 6, 3, 7]
P_AT = [128 * (T * j - j * (j - 1) // 2) for j in range(T + 1)]

DVE_STEPS = 49


def adaln_block(nc, x, w_qk_t, b_q, b_k, lepe_w, lepe_b, w_q, w_k, w_gate, v_exp, o_exp, c_t, w_mod, consts, out):
    f32, bf16, u32 = mybir.dt.float32, mybir.dt.bfloat16, mybir.dt.uint32
    ALU, ACT, AX = mybir.AluOpType, mybir.ActivationFunctionType, mybir.AxisListType

    ctx = ExitStack()
    with ctx:
        def sb(name, shape, dt=f32):
            return ctx.enter_context(nc.sbuf_tensor(name, shape, dt))

        per_batch = {}

        def sem(name, per=0):
            made = ctx.enter_context(nc.semaphore(name))
            per_batch[id(made)] = per
            return made

        def tiles(ap, w=C):
            return ap.rearrange("p (t c) -> p t c", c=w)

        weights_loaded = sem("weights_loaded")
        silu_exp_ready = sem("silu_exp_ready")
        silu_ready = sem("silu_ready")
        mod_ps_ready = sem("mod_ps_ready")
        setup_ready = sem("setup_ready")
        wait_carried = sem("wait_carried")
        x_loaded = sem("x_loaded", 16)
        mod_picked = sem("mod_picked", 1)
        var_ready = sem("var_ready", 2)
        rstd_ready = sem("rstd_ready", 2)
        xn_ready = sem("xn_ready", 2 * T)
        xnT_ps = sem("xnT_ps", 2)
        hT_ready = sem("hT_ready", 1)
        h2T_ready = sem("h2T_ready", 1)
        hn_ps = sem("hn_ps", 1)
        hn_ready = sem("hn_ready", 1)
        q_ps = sem("q_ps", 1)
        k_ps = sem("k_ps", 1)
        qmin_ready = sem("qmin_ready", 1)
        kmin_ready = sem("kmin_ready", 1)
        qexp_ready = sem("qexp_ready", 1)
        kexp_ready = sem("kexp_ready", 1)
        qT_ready = sem("qT_ready", 1)
        k_ready = sem("k_ready", 1)
        conv_mid = sem("conv_mid", 1)
        conv_ready = sem("conv_ready", 1)
        kv_ps = sem("kv_ps", 1)
        kv_ready = sem("kv_ready", 1)
        kmean_ready = sem("kmean_ready", 1)
        rkv_ps = sem("rkv_ps", 1)
        rkv_ready = sem("rkv_ready", 1)
        rrkv_ps = sem("rrkv_ps", 1)
        rrkv_ready = sem("rrkv_ready", 1)
        att_ps = sem("att_ps", 1)
        conv_ps = sem("conv_ps", 1)
        x1_ready = sem("x1_ready", 1)
        logit_ps = sem("logit_ps", 1)
        top_ready = sem("top_ready", 1)
        topexp_ready = sem("topexp_ready", 1)
        gate_ready = sem("gate_ready", 1)
        mask_ready = sem("mask_ready", 1)
        proj_ps = sem("proj_ps", 2 * HP)
        proj_ready = sem("proj_ready", 2 * HP)
        val_ps = sem("val_ps", T * E)
        val_first = sem("val_first", T)
        val_picked = sem("val_picked", T * (E - 1))
        val_ready = sem("val_ready", T)
        max_ps = sem("max_ps", T * H)
        max_ready = sem("max_ready", T * H)
        maxrow_ps = sem("maxrow_ps", H)
        maxrow_ready = sem("maxrow_ready", H)
        maxrow_in = sem("maxrow_in", 16 * H)
        score_ps = sem("score_ps", T * H)
        prob_ready = sem("prob_ready", T * H)
        av_ps = sem("av_ps", 2 * H)
        o_ready = sem("o_ready", 2 * H)
        selT_ps = sem("selT_ps", 1)
        selT_ready = sem("selT_ready", 1)
        oT_ps = sem("oT_ps", HP)
        oT_ready = sem("oT_ready", H)
        selB_ps = sem("selB_ps", H)
        z_ready = sem("z_ready", H * EC)
        z_used = sem("z_used", H * EC)
        yT_ready = sem("yT_ready", 1)
        y_ps = sem("y_ps", 1)
        out_ready = sem("out_ready", 1)
        out_stored = sem("out_stored", 16)
        dve_step = sem("dve_step", DVE_STEPS)
        one_ahead = {"yT_ready": yT_ready, "out_ready": out_ready, "out_stored": out_stored, "z_ready": z_ready}

        kept = sum(list(CONSTS.values())[:KEPT])
        cst = sb("cst", [128, kept])

        def const(name, rows=128):
            at, tensor = CONST_AT[name], cst
            if at >= kept:
                at, tensor = at - kept, cst_once
            return tensor[0:rows, at:at + CONSTS[name]]

        ident = const("ident")
        wqk_sb = sb("wqk_sb", [C, 2 * C])
        bq_sb, bk_sb = sb("bq_sb", [C, 1]), sb("bk_sb", [1, C])
        bq1_sb = sb("bq1_sb", [C, 1])
        lw_sb, lb_sb = sb("lw_sb", [C, 3]), sb("lb_sb", [C, 1])
        wq_sb, wk_sb = sb("wq_sb", [C, H * K]), sb("wk_sb", [C, H * K])
        wg_sb = sb("wg_sb", [C, H * E])
        v_w = sb("v_w", [C, E, H * K])
        o_w = sb("o_w", [128, H * EC, C])
        cT_sb, sig_sb, silu_sb = sb("cT_sb", [C, B]), sb("sig_sb", [C, B]), sb("silu_sb", [C, B])
        mod_sb = sb("mod_sb", [C, 6, B])
        ga_row = sb("ga_row", [128, B, C])
        ident_b = sb("ident_b", [128, 128], bf16)
        causal_b, causal_tb = sb("causal_b", [128, 128], bf16), sb("causal_tb", [128, 128], bf16)
        row_of_b = sb("row_of_b", [H, H * 128], bf16)
        ones_sb = sb("ones_sb", [1, 128])
        half_sb = sb("half_sb", [128, T])

        x_sb, x1_sb = sb("x_sb", [128, T, C]), sb("x1_sb", [128, T, C])
        modb = sb("modb", [C, 6])
        stats, mv, ve = sb("stats", [128, T, 6]), sb("mv", [128, T, 2]), sb("ve", [128, T])
        rstd = sb("rstd", [128, T])
        p_sb = sb("p_sb", [128, 2, P_AT[T]])
        spare = p_sb[:, :, :].rearrange("p a n -> p (a n)")
        xn, att = tiles(spare[:, 0:N]), tiles(spare[:, N:2 * N])
        conv = yT = spare[:, 2 * N:3 * N]
        lg, eq, mask = (spare[:, 3 * N + i * N // 2:3 * N + (i + 1) * N // 2].rearrange("p (t e) -> p t e", e=E)
                        for i in range(3))
        hT = sb("hT", [C, N + 2])
        h2T = sb("h2T", [C, N])
        out_sb = tiles(h2T[:])
        v_sb = sb("v_sb", [128, T, H, K + 1])
        hn = v_sb[:, :, :, :].rearrange("p t h k -> p (t h k)")[:, 0:T * (C + 1)].rearrange(
            "p (t c) -> p t c", c=C + 1)
        o_sb = sb("o_sb", [128, T, H, K])
        qT = o_sb[:, 0:2, :, :].rearrange("p t h k -> p (t h k)")
        qe = o_sb[:, 2:4, :, :].rearrange("p t h k -> p (t h k)")
        ke = o_sb[:, 4:6, :, :].rearrange("p t h k -> p (t h k)")
        kn = o_sb[:, 6:8, :, :].rearrange("p t h k -> p (t h k)")
        qh_all = sb("qh", [128, H, N])
        qh = qh_all[0:K + 1]
        kh = sb("kh", [K + 1, H, N])
        qb, kb = (a[0:K].bitcast(bf16).rearrange("k h (n two) -> k h n two", two=2)[:, :, :, 1] for a in (qh, kh))
        z, oT = qh_all[:, 0:4], qh_all[:, 4:8]
        wmod_sb, sign_sb = qh_all[:, 7, 0:6 * C], qh_all[:, 6, 0:B * C]
        cst_once = qh_all[:, 0:2, :].rearrange("p h n -> p (h n)")[:, 0:sum(CONSTS.values()) - kept]

        def wmod_view(m):
            return wmod_sb[:, m * C:(m + 1) * C]
        kv_sb, rkv_sb = sb("kv_sb", [C, C]), sb("rkv_sb", [C, C])
        kvz = sb("kvz", [C, C + LH])
        ksum = sb("ksum", [C, 1])
        den = sb("den", [128, T * LH])
        top, best, sel = sb("top", [128, T * H]), sb("best", [128, T * H]), sb("sel", [128, T * H])
        gate = sb("gate", [128, T * H])
        m8, mrow = sb("m8", [128, 2, T]), sb("mrow", [T, 2, 128])
        rden = sb("rden", [128, 2, 4])
        selT = sb("selT", [H, N], bf16)
        PS = ctx.enter_context(nc.psum_tensor("PS", [128, 8 * 512], f32))

        def bank(i, n=1):
            return PS[:, i * 512:(i + n) * 512]

        block = ctx.enter_context(nc.Block())

        class Counts:

            def __init__(self, eng, first=0):
                self.eng, self.held, self.start = eng, None, {}
                self.target = eng.alloc_register(f"{eng.engine.name}_target")
                for per in sorted({p for p in per_batch.values() if p}):
                    self.start[per] = eng.alloc_register(f"{eng.engine.name}_start_{per}")
                    eng.reg_mov(self.start[per], first * per)

            def __call__(self, sem, count):
                per = per_batch[id(sem)]
                count += any(sem is s for s in one_ahead.values())
                assert count > 0
                if self.held != (per, count):
                    self.eng.reg_add(self.target, self.start[per], count)
                    self.held = (per, count)
                return self.target

            def next_batch(self):
                self.held = None
                for per, register in self.start.items():
                    self.eng.reg_add(register, register, per)

        @block.sync
        def _(sp):
            x_v = x.rearrange("b (t p) c -> b p t c", p=128)
            out_v = out.rearrange("b (t p) c -> b p t c", p=128)
            sp.dma_start(x_sb[:], x_v[0, :, :, :]).then_inc(x_loaded, 16)
            for dst, src in ((cst[:], consts[:, 0:kept]), (cst_once, consts[:, kept:]), (cT_sb[:], c_t), (wqk_sb[:], w_qk_t), (bq_sb[:], b_q),
                             (bk_sb[:], b_k), (lw_sb[:], lepe_w), (lb_sb[:], lepe_b), (wg_sb[:], w_gate),
                             (wmod_sb, w_mod), (wq_sb[:], w_q), (wk_sb[:], w_k), (v_w[:], v_exp), (o_w[:], o_exp)):
                sp.dma_start(dst, src).then_inc(weights_loaded, 16)

            def batch(b, more):
                if more:
                    sp.wait_ge(x1_ready, upto(x1_ready, 1))
                    up = sp.dma_start(x_sb[:], x_v[b + 1, :, :, :])
                    up.then_inc(x_loaded, 16)
                for h in range(H):
                    sp.wait_ge(maxrow_ready, upto(maxrow_ready, h + 1))
                    sp.dma_start(qh[K:K + 1, h, :], mrow[:, h % 2, :]).then_inc(maxrow_in, 16)
                sp.wait_ge(out_ready, upto(out_ready, 1))
                sp.dma_start(out_v[b, :, :, :], out_sb[:]).then_inc(out_stored, 16)

            upto = Counts(sp)
            with sp.Fori(0, B - 1) as b:
                batch(b, True)
                upto.next_batch()
            batch(B - 1, False)
            sp.wait_ge(out_stored, 16 * B + 1)

        @block.gpsimd
        def _(pool):
            upto = Counts(pool)
            with pool.Fori(0, B) as b:
                for k in range(2):
                    pool.wait_ge(var_ready, upto(var_ready, k + 1))
                    nc.gpsimd.tensor_tensor(rstd[:], ve[:], half_sb[:], ALU.pow).then_inc(rstd_ready, 1)
                pool.wait_ge(gate_ready, upto(gate_ready, 1))
                for t in range(T):
                    pool.wait_ge(val_picked, upto(val_picked, (E - 1) * (t + 1)))
                    v_t = v_sb[:, t, :, 0:K]
                    g_t = gate[:, t * H:(t + 1) * H].unsqueeze(2).broadcast_to([128, H, K])
                    nc.gpsimd.tensor_tensor(v_t, v_t, g_t, ALU.mult).then_inc(val_ready, 1)
                upto.next_batch()

        @block.scalar
        def _(act):
            act.wait_ge(weights_loaded, 16 * 14)
            nc.scalar.activation(sig_sb[:], cT_sb[:], ACT.Exp, scale=-1.0).then_inc(silu_exp_ready, 1)
            act.wait_ge(setup_ready, 1)
            upto = Counts(act)
            with act.Fori(0, B) as b:
                act.wait_ge(xnT_ps, upto(xnT_ps, 1))
                act.wait_ge(mod_picked, upto(mod_picked, 1))
                nc.scalar.activation(hT[:, 1:N + 1], bank(0, 2), ACT.Identity,
                                                      scale=modb[:, MOD_CA:MOD_CA + 1],
                                                      bias=modb[:, MOD_SA:MOD_SA + 1]).then_inc(hT_ready, 1)
                act.wait_ge(hT_ready, upto(hT_ready, 1))
                nc.scalar.activation(conv[:], hT[:, 1:N + 1], ACT.Identity,
                                                      scale=lw_sb[:, 1:2], bias=lb_sb[:]).then_inc(conv_mid, 1)
                act.wait_ge(kmin_ready, upto(kmin_ready, 1))
                nc.scalar.activation(ke, ke, ACT.Exp).then_inc(kexp_ready, 1)
                act.wait_ge(qmin_ready, upto(qmin_ready, 1))
                nc.scalar.activation(qe, qe, ACT.Exp).then_inc(qexp_ready, 1)
                act.wait_ge(xnT_ps, upto(xnT_ps, 2))
                act.wait_ge(out_stored, upto(out_stored, 0))
                nc.scalar.activation(h2T[:], bank(0, 2), ACT.Identity,
                                                       scale=modb[:, MOD_CB:MOD_CB + 1],
                                                       bias=modb[:, MOD_SB:MOD_SB + 1]).then_inc(h2T_ready, 1)
                act.wait_ge(top_ready, upto(top_ready, 1))
                nc.scalar.activation(gate[:], top[:], ACT.Exp, scale=-1.0).then_inc(topexp_ready, 1)
                for t in range(T):
                    act.wait_ge(proj_ps, upto(proj_ps, t + 1))
                    src, dst = bank(4 + 2 * (t % 2), 2), (qh, kh)[t % 2]
                    nc.scalar.activation(dst[0:K, t // 2 * 2, :], src[0:K], ACT.Copy)
                    nc.scalar.activation(dst[0:K, t // 2 * 2 + 1, :], src[K:2 * K], ACT.Copy).then_inc(proj_ready, 1)
                    act.wait_ge(val_ps, upto(val_ps, E * t + 1))
                    nc.scalar.activation(v_sb[:, t, :, 0:K], tiles(bank(E * t % 4), K), ACT.Copy).then_inc(val_first, 1)
                for h in range(H):
                    if h >= 2:
                        act.wait_ge(av_ps, upto(av_ps, 2 * (h - 1)))
                    for n, j in enumerate(KEY_ORDER):
                        act.wait_ge(score_ps, upto(score_ps, T * h + n + 1))
                        src = bank(3, 2)[:, 128 * j:N] if j < 4 else bank(5)[:, 128 * (j - 4):512]
                        nc.scalar.activation(p_sb[:, h % 2, P_AT[j]:P_AT[j + 1]], src, ACT.Exp,
                                                                scale=SCALE).then_inc(prob_ready, 1)
                act.wait_ge(selT_ps, upto(selT_ps, 1))
                nc.scalar.activation(selT[:], bank(6, 2)[0:H], ACT.Copy).then_inc(selT_ready, 1)
                for h in range(H):
                    act.wait_ge(oT_ps, upto(oT_ps, h // 2 + 1))
                    if h >= 4:
                        act.wait_ge(z_ready, upto(z_ready, EC * (h - 3)))
                    src = bank(2, 2)[K * (h % 2):K * (h % 2 + 1)]
                    nc.scalar.activation(oT[0:K, h % 4, :], src, ACT.Copy)
                    nc.scalar.activation(oT[K:2 * K, h % 4, :], src, ACT.Copy).then_inc(oT_ready, 1)
                act.wait_ge(z_used, upto(z_used, H * EC))
                nc.scalar.activation(yT[:], bank(0, 2), ACT.Copy,
                                                      scale=modb[:, MOD_GB:MOD_GB + 1]).then_inc(yT_ready, 1)
                upto.next_batch()

        @block.vector
        def _(dve):
            v = nc.vector

            steps = [0]
            for ahead in one_ahead.values():
                dve.sem_inc(ahead, 1)

            def link0(ins):
                steps[0] += 1
                ins.then_inc(dve_step, 1)
                dve.wait_ge(dve_step, steps[0])

            v.memset(hT[:, 0:1], 0.0)
            v.memset(hT[:, N + 1:N + 2], 0.0)
            v.memset(kh[K:K + 1, :, :], 1.0)
            v.memset(ones_sb[:], 1.0)
            v.memset(half_sb[:], -0.5)
            dve.wait_ge(weights_loaded, 16 * 14)
            v.tensor_copy(ident_b[:], ident)
            v.tensor_copy(causal_b[:], const("causal"))
            v.tensor_copy(causal_tb[:], const("causal_t"))
            v.tensor_copy(row_of_b[:], const("row_of", H))
            v.tensor_scalar(bq1_sb[:], bq_sb[:], 1.0, None, ALU.add)
            dve.wait_ge(silu_exp_ready, 1)
            link0(v.tensor_scalar(sig_sb[:], sig_sb[:], 1.0, None, ALU.add))
            link0(v.reciprocal(sig_sb[:], sig_sb[:]))
            v.tensor_tensor(silu_sb[:], sig_sb[:], cT_sb[:], ALU.mult).then_inc(silu_ready, 1)
            dve.wait_ge(mod_ps_ready, 1)
            link0(v.tensor_copy(mod_sb[:].rearrange("p m b -> p (m b)"), bank(0)[:, 0:6 * B]))
            for m in (MOD_CA, MOD_CB):
                link0(v.tensor_scalar(mod_sb[:, m, :], mod_sb[:, m, :], 1.0, None, ALU.add))
            link0(v.tensor_copy(ga_row[:].rearrange("p b c -> p (b c)"), bank(1)))

            def clamp(ap, sign):
                link0(v.tensor_scalar(sign, ap, 0.0, 2.0, ALU.is_ge, ALU.mult))
                link0(v.tensor_scalar(sign, sign, -1.0, None, ALU.add))
                link0(v.tensor_tensor(ap, ap, sign, ALU.mult))
                link0(v.tensor_scalar(ap, ap, 0.25, None, ALU.max))
                link0(v.tensor_tensor(ap, ap, sign, ALU.mult))

            clamp(mod_sb[:, MOD_GB, :], sign_sb[:, 0:B])
            clamp(ga_row[:].rearrange("p b c -> p (b c)"), sign_sb[:])
            v.memset(ve[:], 1.0).then_inc(setup_ready, 1)
            dve.wait_ge(setup_ready, 1)
            base = steps[0]

            upto = Counts(dve)
            with dve.Fori(0, B) as b:
                links = [0]

                def link(ins):
                    links[0] += 1
                    ins.then_inc(dve_step, 1)
                    dve.wait_ge(dve_step, upto(dve_step, base + links[0]))

                def normalise(src, k):
                    for t in range(T):
                        last = v.bn_stats(stats[:, t, :], src[:, t, :])
                    link(last)
                    dve.sem_inc(wait_carried, 1)
                    for t in range(T):
                        last = v.bn_aggr(mv[:, t, :], stats[:, t, :])
                    link(last)
                    v.tensor_scalar(ve[:], mv[:, :, 1], EPS, None, ALU.add).then_inc(var_ready, 1)
                    dve.wait_ge(rstd_ready, upto(rstd_ready, k + 1))
                    for t in range(T):
                        v.tensor_scalar(xn[:, t, :], src[:, t, :], mv[:, t, 0:1], rstd[:, t:t + 1],
                                                         ALU.subtract, ALU.mult).then_inc(xn_ready, 1)

                dve.wait_ge(yT_ready, upto(yT_ready, 0))
                v.tensor_copy(modb[:], mod_sb[:, :, bass.ds(b, 1)].rearrange("p m b -> p (m b)")).then_inc(mod_picked, 1)
                dve.wait_ge(x_loaded, upto(x_loaded, 16))
                normalise(x_sb, 0)

                dve.wait_ge(hn_ps, upto(hn_ps, 1))
                v.tensor_copy(hn[:, :, 0:C], tiles(bank(2, 2)))
                v.memset(hn[:, :, C:C + 1], 1.0).then_inc(hn_ready, 1)
                dve.wait_ge(k_ps, upto(k_ps, 1))
                v.tensor_scalar(ke, bank(6, 2), 0.0, None, ALU.min).then_inc(kmin_ready, 1)
                dve.wait_ge(q_ps, upto(q_ps, 1))
                v.tensor_scalar(qe, bank(4, 2), bq_sb[:], 0.0, ALU.add, ALU.min).then_inc(qmin_ready, 1)
                dve.wait_ge(kexp_ready, upto(kexp_ready, 1))
                v.scalar_tensor_tensor(kn, bank(6, 2), 1.0, ke, ALU.add, ALU.max).then_inc(k_ready, 1)
                dve.wait_ge(qexp_ready, upto(qexp_ready, 1))
                v.scalar_tensor_tensor(qT, bank(4, 2), bq1_sb[:], qe, ALU.add, ALU.max).then_inc(qT_ready, 1)
                dve.wait_ge(kv_ps, upto(kv_ps, 1))
                v.tensor_tensor(kv_sb[:], bank(0)[:, 0:C], const("same_head"), ALU.mult).then_inc(kv_ready, 1)
                link(v.tensor_copy(ksum[:], bank(0)[:, C:C + 1]))
                v.tensor_scalar(kvz[:, C:C + LH], const("head_of"), ksum[:], None, ALU.mult).then_inc(kmean_ready, 1)
                dve.wait_ge(rkv_ps, upto(rkv_ps, 1))
                v.tensor_copy(rkv_sb[:], bank(1)[:, 0:C]).then_inc(rkv_ready, 1)
                dve.wait_ge(rrkv_ps, upto(rrkv_ps, 1))
                v.tensor_copy(kvz[:, 0:C], bank(0)[:, 0:C]).then_inc(rrkv_ready, 1)
                dve.wait_ge(conv_mid, upto(conv_mid, 1))
                link(v.scalar_tensor_tensor(conv[:], hT[:, 0:N], lw_sb[:, 0:1], conv[:], ALU.mult, ALU.add))
                v.scalar_tensor_tensor(conv[:], hT[:, 2:N + 2], lw_sb[:, 2:3], conv[:],
                                                          ALU.mult, ALU.add).then_inc(conv_ready, 1)
                dve.wait_ge(att_ps, upto(att_ps, 1))
                link(v.tensor_scalar(den[:], bank(4)[:, 0:T * LH], 1e-6, None, ALU.add))
                link(v.reciprocal(den[:], den[:]))
                att_h = att[:].rearrange("p t (h d) -> p (t h) d", d=LD)
                link(v.tensor_tensor(att_h, tiles(bank(2, 2), LD), den[:].unsqueeze(2).broadcast_to([128, T * LH, LD]),
                                     ALU.mult))
                dve.wait_ge(conv_ps, upto(conv_ps, 1))
                link(v.tensor_tensor(att[:], att[:], tiles(bank(6, 2)), ALU.add))
                link(v.tensor_tensor(att[:], att[:], ga_row[:, bass.ds(b, 1), :].broadcast_to([128, T, C]), ALU.mult))
                v.tensor_tensor(x1_sb[:], att[:], x_sb[:], ALU.add).then_inc(x1_ready, 1)
                dve.wait_ge(x1_ready, upto(x1_ready, 1))
                normalise(x1_sb, 1)

                dve.wait_ge(logit_ps, upto(logit_ps, 1))
                link(v.tensor_scalar(lg[:], tiles(bank(2), E), SATURATED, None, ALU.min))
                v.tensor_reduce(top[:], lg[:], AX.X, ALU.max).then_inc(top_ready, 1)
                dve.wait_ge(top_ready, upto(top_ready, 1))
                link(v.tensor_tensor(eq[:], lg[:], top[:].unsqueeze(2).broadcast_to([128, T * H, E]), ALU.is_equal))
                link(v.tensor_tensor(eq[:], eq[:], const("rank").unsqueeze(1).broadcast_to([128, T * H, E]), ALU.mult))
                link(v.tensor_reduce(best[:], eq[:], AX.X, ALU.max))
                v.tensor_scalar(sel[:], best[:], -1.0, float(E), ALU.mult, ALU.add)
                link(v.tensor_tensor(mask[:], eq[:], best[:].unsqueeze(2).broadcast_to([128, T * H, E]), ALU.is_equal))
                dve.wait_ge(topexp_ready, upto(topexp_ready, 1))
                link(v.tensor_scalar(gate[:], gate[:], 1.0, None, ALU.add))
                v.reciprocal(gate[:], gate[:]).then_inc(gate_ready, 1)

                for t in range(T):
                    dve.wait_ge(val_first, upto(val_first, t + 1))
                    for e in range(1, E):
                        dve.wait_ge(val_ps, upto(val_ps, E * t + e + 1))
                        dve.sem_inc(wait_carried, 1)
                        pick = mask[:, t * H:(t + 1) * H, e:e + 1].bitcast(u32).broadcast_to([128, H, K])
                        v.copy_predicated(v_sb[:, t, :, 0:K], pick, tiles(bank((E * t + e) % 4), K)).then_inc(val_picked, 1)
                        dve.wait_ge(val_picked, upto(val_picked, (E - 1) * t + e))
                S_ones = v.memset(v_sb[:, :, :, K:K + 1], 1.0)
                S_ones.then_inc(mask_ready, 1)

                def maxima(h, ns):
                    for n in ns:
                        t = MAX_ORDER[n]
                        dve.wait_ge(max_ps, upto(max_ps, T * h + n + 1))
                        src = bank(1, 2)[:, 0:128 * (t + 1)] if t >= 4 else bank(0)[:, 0:128 * (t + 1)]
                        v.tensor_reduce(m8[:, h % 2, t:t + 1], src, AX.X, ALU.max).then_inc(max_ready, 1)

                def max_row(h):
                    dve.wait_ge(maxrow_ps, upto(maxrow_ps, h + 1))
                    if h >= 2:
                        dve.wait_ge(maxrow_in, upto(maxrow_in, 16 * (h - 1)))
                    v.tensor_scalar(mrow[:, h % 2, :], bank(0)[0:T, 0:128], -1.0, None,
                                                         ALU.mult).then_inc(maxrow_ready, 1)

                def heads_out(h, half):
                    dve.wait_ge(av_ps, upto(av_ps, 2 * h + half + 1))
                    src = bank(6 + half)[:, 0:4 * (K + 1)].rearrange("p (t k) -> p t k", k=K + 1)
                    link(v.reciprocal(rden[:, half, :], src[:, :, K]))
                    g = gate[:].rearrange("p (t h) -> p t h", h=H)[:, 4 * half:4 * half + 4, h]
                    link(v.tensor_tensor(rden[:, half, :], rden[:, half, :], g, ALU.mult))
                    v.tensor_tensor(o_sb[:, 4 * half:4 * half + 4, h, :], src[:, :, 0:K],
                                                    rden[:, half, :].unsqueeze(2).broadcast_to([128, 4, K]), ALU.mult).then_inc(o_ready, 1)

                maxima(0, range(T))
                max_row(0)
                for h in range(H + 1):
                    if h + 1 < H:
                        maxima(h + 1, range(4))
                        maxima(h + 1, range(4, T))
                    if h >= 1:
                        heads_out(h - 1, 0)
                    if h + 1 < H:
                        max_row(h + 1)
                    if h >= 1:
                        heads_out(h - 1, 1)

                for h in range(H):
                    dve.wait_ge(oT_ready, upto(oT_ready, h + 1))
                    dve.wait_ge(selB_ps, upto(selB_ps, h + 1))
                    for c in range(EC):
                        n = EC * h + c
                        if n >= 4:
                            dve.wait_ge(z_used, upto(z_used, n - 3))
                        v.scalar_tensor_tensor(z[:, n % 4, :], bank(4 + 2 * (h % 2), 2),
                                                               const("expert_of")[:, c:c + 1], oT[:, h % 4, :],
                                                               ALU.is_equal, ALU.mult).then_inc(z_ready, 1)
                dve.wait_ge(y_ps, upto(y_ps, 1))
                dve.wait_ge(out_stored, upto(out_stored, 0))
                v.tensor_tensor(out_sb[:], x1_sb[:], tiles(bank(2, 2)), ALU.add).then_inc(out_ready, 1)
                assert links[0] == DVE_STEPS, links[0]
                upto.next_batch()

        @block.tensor
        def _(pe):
            mm = nc.tensor.matmul
            pe.wait_ge(silu_ready, 1)
            for m in range(6):
                mm(bank(0)[:, m * B:(m + 1) * B], wmod_view(m), silu_sb[:], start=True, stop=True)
            for i in range(B):
                last = mm(bank(1)[:, i * C:(i + 1) * C], silu_sb[:, i:i + 1].broadcast_to([C, 128]), wmod_view(MOD_GA),
                          start=True, stop=True)
            last.then_inc(mod_ps_ready, 1)
            pe.wait_ge(setup_ready, 1)

            upto = Counts(pe)
            with pe.Fori(0, B) as b:
                def transpose_tiles(first, src, signal, width=128, waits=None):
                    for t in range(T):
                        if waits:
                            waits(t)
                        last = nc.tensor.transpose(bank(first, 2)[0:width, t * 128:(t + 1) * 128], src(t), ident)
                    last.then_inc(signal, 1)

                pe.wait_ge(yT_ready, upto(yT_ready, 0))
                pe.wait_ge(out_ready, upto(out_ready, 0))
                pe.wait_ge(z_ready, upto(z_ready, 0))
                transpose_tiles(0, lambda t: xn[:, t, :], xnT_ps, waits=lambda t: pe.wait_ge(xn_ready, upto(xn_ready, t + 1)))
                pe.wait_ge(hT_ready, upto(hT_ready, 1))
                transpose_tiles(2, lambda t: hT[:, 1 + t * 128:1 + (t + 1) * 128], hn_ps)
                for i in range(2):
                    mm(bank(6 + i), ones_sb[:], bk_sb[:].unsqueeze(1).broadcast_to([1, 4, C]), start=True, stop=True)
                    for t in range(4):
                        n = 4 * i + t
                        last = mm(bank(6 + i)[:, t * C:(t + 1) * C], hT[:, 1 + n * 128:1 + (n + 1) * 128],
                                  wqk_sb[:, C:2 * C], start=False, stop=True, skip_group_check=True)
                last.then_inc(k_ps, 1)
                for i in range(2):
                    last = mm(bank(4 + i), wqk_sb[:, 0:C], hT[:, 1 + i * 512:1 + (i + 1) * 512], start=True, stop=True)
                last.then_inc(q_ps, 1)
                pe.wait_ge(hn_ready, upto(hn_ready, 1))
                pe.wait_ge(k_ready, upto(k_ready, 1))
                for t in range(T):
                    last = mm(bank(0)[:, 0:C + 1], kn[:, t * C:(t + 1) * C], hn[:, t, :], start=t == 0, stop=t == T - 1)
                last.then_inc(kv_ps, 1)
                pe.wait_ge(kv_ready, upto(kv_ready, 1))
                mm(bank(1)[:, 0:C], const("rot_t"), kv_sb[:], start=True, stop=True).then_inc(rkv_ps, 1)
                pe.wait_ge(rkv_ready, upto(rkv_ready, 1))
                pe.wait_ge(kmean_ready, upto(kmean_ready, 1))
                mm(bank(0)[:, 0:C], const("rot"), rkv_sb[:], start=True, stop=True).then_inc(rrkv_ps, 1)
                pe.wait_ge(rrkv_ready, upto(rrkv_ready, 1))
                pe.wait_ge(qT_ready, upto(qT_ready, 1))
                for t in range(T):
                    mm(bank(2, 2)[:, t * C:(t + 1) * C], qT[:, t * 128:(t + 1) * 128], kvz[:, 0:C],
                       start=True, stop=True)
                    last = mm(bank(4)[:, t * LH:(t + 1) * LH], qT[:, t * 128:(t + 1) * 128], kvz[:, C:C + LH],
                              start=True, stop=True)
                last.then_inc(att_ps, 1)
                pe.wait_ge(conv_ready, upto(conv_ready, 1))
                transpose_tiles(6, lambda t: conv[:, t * 128:(t + 1) * 128], conv_ps)
                transpose_tiles(0, lambda t: xn[:, t, :], xnT_ps,
                                waits=lambda t: pe.wait_ge(xn_ready, upto(xn_ready, T + t + 1)))

                pe.wait_ge(h2T_ready, upto(h2T_ready, 1))
                for t in range(T):
                    last = mm(bank(2)[:, t * H * E:(t + 1) * H * E], h2T[:, t * 128:(t + 1) * 128], wg_sb[:],
                              start=True, stop=True)
                last.then_inc(logit_ps, 1)
                for t in range(T):
                    if t >= 2:
                        pe.wait_ge(proj_ready, upto(proj_ready, t - 1))
                    w = (wq_sb, wk_sb)[t % 2][:, t // 2 * 128:(t // 2 + 1) * 128]
                    for i in range(2):
                        last = mm(bank(4 + 2 * (t % 2) + i), w, h2T[:, i * 512:(i + 1) * 512], start=True, stop=True)
                    last.then_inc(proj_ps, 1)
                    for e in range(E):
                        n = E * t + e
                        if n == 2:
                            pe.wait_ge(top_ready, upto(top_ready, 1))
                        if n >= 4:
                            t4, e4 = divmod(n - 4, E)
                            if e4:
                                pe.wait_ge(val_picked, upto(val_picked, (E - 1) * t4 + e4))
                            else:
                                pe.wait_ge(val_first, upto(val_first, t4 + 1))
                        mm(bank(n % 4), h2T[:, t * 128:(t + 1) * 128], v_w[:, e, :],
                                          start=True, stop=True).then_inc(val_ps, 1)

                def max_tile(h, n):
                    t = MAX_ORDER[n]
                    if n >= 2:
                        pe.wait_ge(max_ready, upto(max_ready, T * h + n - 1))
                    elif h:
                        pe.wait_ge(max_ready, upto(max_ready, T * h))
                        pe.wait_ge(maxrow_ready, upto(maxrow_ready, h))
                    dst = bank(1, 2) if t >= 4 else bank(0)
                    q = qb[:, h, t * 128:(t + 1) * 128]
                    w = 128 * (t + 1)
                    for at in range(0, w, 512):
                        to = min(at + 512, w)
                        mm(dst[:, at:to], q, kb[:, h, at:to], start=True, stop=True)
                    mm(dst[:, w - 128:w], ident_b[:], causal_b[:], start=False, stop=True,
                                       skip_group_check=True).then_inc(max_ps, 1)

                def max_row(h):
                    pe.wait_ge(max_ready, upto(max_ready, T * (h + 1)))
                    nc.tensor.transpose(bank(0)[0:T, 0:128], m8[:, h % 2, :], ident).then_inc(maxrow_ps, 1)

                def score_tile(h, n):
                    j = KEY_ORDER[n]
                    if n >= 2:
                        pe.wait_ge(prob_ready, upto(prob_ready, T * h + n - 1))
                    else:
                        if h:
                            pe.wait_ge(prob_ready, upto(prob_ready, T * h))
                        pe.wait_ge(maxrow_in, upto(maxrow_in, 16 * (h + 1)))
                    dst, off = (bank(3, 2), 0) if j < 4 else (bank(5), 512)
                    k = kh[:, h, j * 128:(j + 1) * 128]
                    edge = max(512, 128 * (j + 1)) if j < 4 else N
                    for at, to in ((128 * j, edge), (edge, N)):
                        if at == to:
                            continue
                        last = mm(dst[:, at - off:to - off], k, qh[:, h, at:to], start=True, stop=True)
                        if at == 128 * j:
                            last = mm(dst[:, at - off:at - off + 128], ident_b[:], causal_tb[:], start=False, stop=True,
                                      skip_group_check=True)
                    return last

                def av_tiles(h, s):
                    pe.wait_ge(prob_ready, upto(prob_ready, T * h + (3, 7, 7, 8)[s]))
                    half = s // 2
                    if s % 2 == 0 and h:
                        pe.wait_ge(o_ready, upto(o_ready, 2 * (h - 1) + half + 1))
                    for i in (2 * s, 2 * s + 1):
                        for j in range(i + 1):
                            at = P_AT[j] + 128 * (i - j)
                            last = mm(bank(6 + half)[:, (i % 4) * (K + 1):(i % 4 + 1) * (K + 1)],
                                      p_sb[:, h % 2, at:at + 128], v_sb[:, j, h, :], start=j == 0, stop=j == i)
                    if s % 2:
                        last.then_inc(av_ps, 1)

                pe.wait_ge(val_picked, upto(val_picked, T * (E - 1)))
                pe.wait_ge(val_first, upto(val_first, T))
                pe.wait_ge(proj_ready, upto(proj_ready, 2 * HP))
                for n in range(T):
                    max_tile(0, n)
                max_row(0)
                for h in range(H + 1):
                    for s in range(4):
                        if h + 1 < H and s < 2:
                            for n in range(4 * s, 4 * s + 4):
                                max_tile(h + 1, n)
                        if h >= 1:
                            if h == 1 and s == 0:
                                pe.wait_ge(val_ready, upto(val_ready, T))
                                pe.wait_ge(mask_ready, upto(mask_ready, 1))
                            av_tiles(h - 1, s)
                        if h < H:
                            for n in (2 * s, 2 * s + 1):
                                score_tile(h, n).then_inc(score_ps, 1)
                        if h + 1 < H and s == 2:
                            max_row(h + 1)

                pe.wait_ge(o_ready, upto(o_ready, 2 * H))
                transpose_tiles(6, lambda t: sel[:, t * H:(t + 1) * H], selT_ps, width=H)
                pe.wait_ge(selT_ready, upto(selT_ready, 1))

                def spread(h):
                    if h % 2 == 0:
                        if h:
                            pe.wait_ge(oT_ready, upto(oT_ready, h))
                        transpose_tiles(2, lambda t: o_sb[:, t, h:h + 2, :].rearrange("p h k -> p (h k)"), oT_ps)
                    if h >= 2:
                        pe.wait_ge(z_ready, upto(z_ready, EC * (h - 1)))
                    for i in range(2):
                        last = mm(bank(4 + 2 * (h % 2) + i), row_of_b[:, h * 128:(h + 1) * 128],
                                  selT[:, i * 512:(i + 1) * 512], start=True, stop=True)
                    last.then_inc(selB_ps, 1)

                spread(0)
                for h in range(H):
                    if h + 1 < H:
                        spread(h + 1)
                    for c in range(EC):
                        n = EC * h + c
                        pe.wait_ge(z_ready, upto(z_ready, n + 1))
                        for i in range(2):
                            last = mm(bank(i), o_w[:, n, :], z[:, n % 4, i * 512:(i + 1) * 512],
                                      start=n == 0, stop=n == H * EC - 1)
                        last.then_inc(z_used, 1)
                pe.wait_ge(yT_ready, upto(yT_ready, 1))
                transpose_tiles(2, lambda t: yT[:, t * 128:(t + 1) * 128], y_ps)
                upto.next_batch()


def constants():
    p = np.arange(128)
    theta = (np.float32(1.0) / np.float32(10000.0) ** (np.arange(C // 2, dtype=np.float32) / np.float32(C // 2)))
    cos, sin = np.cos(theta.astype(np.float32)), np.sin(theta.astype(np.float32))
    rot = np.zeros((C, C), np.float32)
    even = 2 * np.arange(C // 2)
    rot[even, even], rot[even, even + 1], rot[even + 1, even], rot[even + 1, even + 1] = cos, -sin, sin, cos
    parts = {
        "ident": np.eye(128),
        "rot": rot, "rot_t": rot.T,
        "same_head": (p[:, None] // LD == p[None, :] // LD) / N,
        "head_of": (p[:, None] // LD == np.arange(LH)[None, :]) / N,
        "rank": np.broadcast_to(E - np.arange(E), (128, E)),
        "expert_of": 2 * np.arange(EC)[None, :] + p[:, None] // K,
        "causal": np.where(p[None, :] > p[:, None], MASKED, 0.0),
        "causal_t": np.where(p[:, None] > p[None, :], MASKED, 0.0),
        "row_of": (p[:, None] == np.arange(H * 128)[None, :] // 128),
    }
    return np.concatenate([np.asarray(parts[n], np.float32) for n in CONSTS], axis=1)


def kernel(L0_attn_x, L0_attn_W_qk, L0_attn_b_qk, L0_attn_lepe_w, L0_attn_lepe_b, L0_ffn_w_q, L0_ffn_w_k,
           L0_ffn_w_gate, L0_ffn_value_experts, L0_ffn_output_experts, L0_c, L0_wmod):
    import concourse.bacc as bacc
    from concourse.bass_utils import run_bass_kernel_spmd

    b_qk = np.asarray(L0_attn_b_qk)
    arrays = dict(
        x=L0_attn_x,
        w_qk_t=np.asarray(L0_attn_W_qk).T,
        b_q=b_qk[:C].reshape(C, 1), b_k=b_qk[C:].reshape(1, C),
        lepe_w=np.asarray(L0_attn_lepe_w).reshape(C, 3), lepe_b=np.asarray(L0_attn_lepe_b).reshape(C, 1),
        w_q=L0_ffn_w_q, w_k=L0_ffn_w_k, w_gate=L0_ffn_w_gate,
        v_exp=np.asarray(L0_ffn_value_experts).transpose(2, 0, 1, 3).reshape(C, E, H * K),
        o_exp=np.asarray(L0_ffn_output_experts).reshape(EC, 2, H, K, C).transpose(1, 3, 2, 0, 4).reshape(
            128, H * EC, C),
        c_t=np.asarray(L0_c).T, w_mod=L0_wmod, consts=constants(),
    )
    arrays = {n: np.ascontiguousarray(a) for n, a in arrays.items()}
    nc = bacc.Bacc("TRN2", target_bir_lowering=False, num_devices=1)
    aps = {n: nc.dram_tensor(n, a.shape, mybir.dt.from_np(a.dtype), kind="ExternalInput").ap()
           for n, a in arrays.items()}
    out = nc.dram_tensor("out", (B, N, C), mybir.dt.float32, kind="ExternalOutput").ap()
    adaln_block(nc, out=out, **aps)
    return run_bass_kernel_spmd(nc, [arrays], core_ids=[0]).results[0]["out"]
```

```python
from contextlib import ExitStack

import numpy as np

import concourse.bass as bass
from concourse import mybir

B, N, C = 4, 1024, 128
T = N // 128
LH = 16
LD = C // LH
H, K, E = 8, 64, 8
HP = H // 2
EC = E * K // 128
SCALE = float(K) ** -0.5
EPS = 1e-5
MASKED = -1e30
SATURATED = 17.0
MOD_SA, MOD_CA, MOD_GA, MOD_SB, MOD_CB, MOD_GB = range(6)

CONSTS = {"ident": C, "rot": C, "rot_t": C, "same_head": C, "head_of": LH, "rank": E, "expert_of": EC,
          "causal": 128, "causal_t": 128, "row_of": H * 128}
KEPT = 7
CONST_AT = {n: sum(list(CONSTS.values())[:i]) for i, n in enumerate(CONSTS)}

MAX_ORDER = [4, 0, 5, 1, 6, 2, 7, 3]
KEY_ORDER = [0, 4, 1, 5, 2, 6, 3, 7]
HEAD_ORDER = [(what, n) for what, ns in (
    ("max", (0, 1)), ("values", (0, 1)), ("score", (0,)), ("values", (2,)), ("score", (1,)),
    ("max", (2, 3)), ("score", (2,)), ("values", (3,)), ("score", (3,)),
    ("max", (4, 5)), ("values", (4,)), ("score", (4, 5)),
    ("max", (6, 7)), ("values", (5,)), ("score", (6, 7)), ("row", (0,)), ("values", (6, 7)),
) for n in ns]
P_AT = [128 * (T * j - j * (j - 1) // 2) for j in range(T + 1)]

SMALL_LOADS = 10
DVE_STEPS = 49


def adaln_block(nc, x, w_qk_t, b_q, b_k, lepe_w, lepe_b, w_q, w_k, w_gate, v_exp, o_exp, c_t, w_mod, consts, out):
    f32, bf16, u32, f32r = mybir.dt.float32, mybir.dt.bfloat16, mybir.dt.uint32, mybir.dt.float32r
    ALU, ACT, AX = mybir.AluOpType, mybir.ActivationFunctionType, mybir.AxisListType

    ctx = ExitStack()
    with ctx:
        def sb(name, shape, dt=f32):
            return ctx.enter_context(nc.sbuf_tensor(name, shape, dt))

        per_batch = {}

        def sem(name, per=0):
            made = ctx.enter_context(nc.semaphore(name))
            per_batch[id(made)] = per
            return made

        def own(h):
            return slice(K * (h % 2), K * (h % 2) + K)

        def other(h):
            return own(h + 1)

        def tiles(ap, w=C):
            return ap.rearrange("p (t c) -> p t c", c=w)

        small_loaded = sem("small_loaded")
        proj_loaded = sem("proj_loaded")
        silu_exp_ready = sem("silu_exp_ready")
        silu_ready = sem("silu_ready")
        mod_ps_ready = sem("mod_ps_ready")
        setup_ready = sem("setup_ready")
        wait_carried = sem("wait_carried")
        x_loaded = sem("x_loaded", 16)
        mod_picked = sem("mod_picked", 1)
        var_ready = sem("var_ready", 2)
        rstd_ready = sem("rstd_ready", 2)
        xn_ready = sem("xn_ready", 2 * T)
        xnT_ps = sem("xnT_ps", 2)
        hT_ready = sem("hT_ready", 1)
        h2T_ready = sem("h2T_ready", 1)
        hn_ps = sem("hn_ps", 1)
        hn_ready = sem("hn_ready", 1)
        q_ps = sem("q_ps", 1)
        k_ps = sem("k_ps", 1)
        qmin_ready = sem("qmin_ready", 1)
        kmin_ready = sem("kmin_ready", 1)
        qexp_ready = sem("qexp_ready", 1)
        kexp_ready = sem("kexp_ready", 1)
        qT_ready = sem("qT_ready", 1)
        k_ready = sem("k_ready", 1)
        conv_mid = sem("conv_mid", 1)
        conv_ready = sem("conv_ready", 1)
        kv_ps = sem("kv_ps", 1)
        kv_ready = sem("kv_ready", 1)
        kmean_ready = sem("kmean_ready", 1)
        rkv_ps = sem("rkv_ps", 1)
        rkv_ready = sem("rkv_ready", 1)
        rrkv_ps = sem("rrkv_ps", 1)
        rrkv_ready = sem("rrkv_ready", 1)
        att_ps = sem("att_ps", 1)
        conv_ps = sem("conv_ps", 1)
        x1_ready = sem("x1_ready", 1)
        logit_ps = sem("logit_ps", 1)
        top_ready = sem("top_ready", 1)
        topexp_ready = sem("topexp_ready", 1)
        gate_ready = sem("gate_ready", 1)
        mask_ready = sem("mask_ready", 1)
        proj_ps = sem("proj_ps", 2 * HP)
        proj_ready = sem("proj_ready", 2 * HP)
        val_ps = sem("val_ps", T * E)
        val_first = sem("val_first", T)
        val_picked = sem("val_picked", T * (E - 1))
        val_ready = sem("val_ready", T)
        max_ps = sem("max_ps", T * H)
        max_ready = sem("max_ready", T * H)
        maxrow_ps = sem("maxrow_ps", H)
        maxrow_ready = sem("maxrow_ready", H)
        maxrow_in = sem("maxrow_in", 16 * H)
        q_hi_ready = sem("q_hi_ready", H)
        k_hi_ready = sem("k_hi_ready", H)
        k_hh_ready = sem("k_hh_ready", H)
        q_lo_ready = sem("q_lo_ready", H)
        q_hm_ready = sem("q_hm_ready", H)
        k_lo_ready = sem("k_lo_ready", H)
        score_ps = sem("score_ps", T * H)
        prob_ready = sem("prob_ready", T * H)
        av_ps = sem("av_ps", 2 * H)
        o_ready = sem("o_ready", 2 * H)
        selT_ps = sem("selT_ps", 1)
        selT_ready = sem("selT_ready", 1)
        oT_ps = sem("oT_ps", HP)
        oT_ready = sem("oT_ready", H)
        selB_ps = sem("selB_ps", H)
        z_ready = sem("z_ready", H * EC)
        z_used = sem("z_used", H * EC)
        yT_ready = sem("yT_ready", 1)
        y_ps = sem("y_ps", 1)
        out_ready = sem("out_ready", 1)
        out_stored = sem("out_stored", 16)
        dve_step = sem("dve_step", DVE_STEPS)
        one_ahead = {"yT_ready": yT_ready, "out_ready": out_ready, "out_stored": out_stored, "z_ready": z_ready}

        kept = sum(list(CONSTS.values())[:KEPT])
        cst = sb("cst", [128, kept])

        def const(name, rows=128):
            at, tensor = CONST_AT[name], cst
            if at >= kept:
                at, tensor = at - kept, cst_once
            return tensor[0:rows, at:at + CONSTS[name]]

        ident = const("ident")
        wqk_sb = sb("wqk_sb", [C, 2 * C])
        bq_sb, bk_sb = sb("bq_sb", [C, 1]), sb("bk_sb", [1, C])
        bq1_sb = sb("bq1_sb", [C, 1])
        lw_sb, lb_sb = sb("lw_sb", [C, 3]), sb("lb_sb", [C, 1])
        wq_sb, wk_sb = sb("wq_sb", [C, H * K]), sb("wk_sb", [C, H * K])
        wg_sb = sb("wg_sb", [C, H * E])
        v_w = sb("v_w", [C, E, H * K])
        o_w = sb("o_w", [128, H * EC, C])
        cT_sb, sig_sb, silu_sb = sb("cT_sb", [C, B]), sb("sig_sb", [C, B]), sb("silu_sb", [C, B])
        mod_sb = sb("mod_sb", [C, 6, B])
        ga_row = sb("ga_row", [128, B, C])
        ident_b = sb("ident_b", [128, 128], bf16)
        causal_b, causal_tb = sb("causal_b", [128, 128], bf16), sb("causal_tb", [128, 128], bf16)
        row_of_b = sb("row_of_b", [H, H * 128], bf16)
        ones_sb = sb("ones_sb", [1, 128])
        half_sb = sb("half_sb", [128, T])

        x_sb, x1_sb = sb("x_sb", [128, T, C]), sb("x1_sb", [128, T, C])
        modb = sb("modb", [C, 6])
        stats, mv, ve = sb("stats", [128, T, 6]), sb("mv", [128, T, 2]), sb("ve", [128, T])
        rstd = sb("rstd", [128, T])
        p_sb = sb("p_sb", [128, 2, P_AT[T]])
        spare = p_sb[:, :, :].rearrange("p a n -> p (a n)")
        xn, att = tiles(spare[:, 0:N]), tiles(spare[:, N:2 * N])
        conv = yT = spare[:, 2 * N:3 * N]
        lg, eq, mask = (spare[:, 3 * N + i * N // 2:3 * N + (i + 1) * N // 2].rearrange("p (t e) -> p t e", e=E)
                        for i in range(3))
        hT = sb("hT", [C, N + 2])
        h2T = sb("h2T", [C, N])
        out_sb = tiles(h2T[:])
        v_sb = sb("v_sb", [128, T, H, K + 1])
        hn = v_sb[:, :, :, :].rearrange("p t h k -> p (t h k)")[:, 0:T * (C + 1)].rearrange(
            "p (t c) -> p t c", c=C + 1)
        o_sb = sb("o_sb", [128, T, H, K])
        qT = o_sb[:, 0:2, :, :].rearrange("p t h k -> p (t h k)")
        qe = o_sb[:, 2:4, :, :].rearrange("p t h k -> p (t h k)")
        ke = o_sb[:, 4:6, :, :].rearrange("p t h k -> p (t h k)")
        kn = o_sb[:, 6:8, :, :].rearrange("p t h k -> p (t h k)")
        qk = sb("qk", [128, 2, HP, N])
        q_hl, k_hh = sb("q_hl", [128, 3, N], f32r), sb("k_hh", [128, 3, N], f32r)
        q_hm, k_l1 = sb("q_hm", [128, 2, N], f32r), sb("k_l1", [128, 2, N], f32r)
        spread_all = qk[:, :, :, :].rearrange("p a h n -> p (a h) n")
        z, oT = spread_all[:, 0:4], spread_all[:, 4:8]
        wmod_sb, sign_sb = spread_all[:, 7, 0:6 * C], spread_all[:, 6, 0:B * C]
        cst_once = spread_all[:, 0:2, :].rearrange("p h n -> p (h n)")[:, 0:sum(CONSTS.values()) - kept]

        def wmod_view(m):
            return wmod_sb[:, m * C:(m + 1) * C]
        kv_sb, rkv_sb = sb("kv_sb", [C, C]), sb("rkv_sb", [C, C])
        kvz = sb("kvz", [C, C + LH])
        ksum = sb("ksum", [C, 1])
        den = sb("den", [128, T * LH])
        top, best, sel = sb("top", [128, T * H]), sb("best", [128, T * H]), sb("sel", [128, T * H])
        gate = sb("gate", [128, T * H])
        m8, mrow = sb("m8", [128, 2, T]), sb("mrow", [T, 2, 128], f32r)
        rden = sb("rden", [128, 2, 4])
        selT = spare[0:H, 0:N // 2].bitcast(bf16)
        PS = ctx.enter_context(nc.psum_tensor("PS", [128, 8 * 512], f32))

        def bank(i, n=1):
            return PS[:, i * 512:(i + n) * 512]

        block = ctx.enter_context(nc.Block())

        class Counts:

            def __init__(self, eng, first=0):
                self.eng, self.held, self.start = eng, None, {}
                self.target = eng.alloc_register(f"{eng.engine.name}_target")
                for per in sorted({p for p in per_batch.values() if p}):
                    self.start[per] = eng.alloc_register(f"{eng.engine.name}_start_{per}")
                    eng.reg_mov(self.start[per], first * per)

            def __call__(self, sem, count):
                per = per_batch[id(sem)]
                count += any(sem is s for s in one_ahead.values())
                assert count > 0
                if self.held != (per, count):
                    self.eng.reg_add(self.target, self.start[per], count)
                    self.held = (per, count)
                return self.target

            def next_batch(self):
                self.held = None
                for per, register in self.start.items():
                    self.eng.reg_add(register, register, per)

        @block.sync
        def _(sp):
            x_v = x.rearrange("b (t p) c -> b p t c", p=128)
            out_v = out.rearrange("b (t p) c -> b p t c", p=128)
            sp.dma_start(x_sb[:], x_v[0, :, :, :]).then_inc(x_loaded, 16)
            small = ((cT_sb[:], c_t), (wmod_sb, w_mod), (cst[:], consts[:, 0:kept]), (cst_once, consts[:, kept:]),
                     (wqk_sb[:], w_qk_t), (bq_sb[:], b_q), (bk_sb[:], b_k), (lw_sb[:], lepe_w), (lb_sb[:], lepe_b),
                     (wg_sb[:], w_gate))
            assert len(small) == SMALL_LOADS
            for dst, src in small:
                sp.dma_start(dst, src).then_inc(small_loaded, 16)
            for dst, src in ((wq_sb[:], w_q), (wk_sb[:], w_k), (v_w[:], v_exp), (o_w[:], o_exp)):
                sp.dma_start(dst, src).then_inc(proj_loaded, 16)

            def batch(b, more):
                if more:
                    sp.wait_ge(x1_ready, upto(x1_ready, 1))
                    up = sp.dma_start(x_sb[:], x_v[b + 1, :, :, :])
                    up.then_inc(x_loaded, 16)
                for h in range(H):
                    sp.wait_ge(maxrow_ready, upto(maxrow_ready, h + 1))
                    sp.dma_start(q_hm[other(h).start:other(h).start + 1, h % 2, :].bitcast(f32),
                                 mrow[:, h % 2, :].bitcast(f32)).then_inc(maxrow_in, 16)
                sp.wait_ge(out_ready, upto(out_ready, 1))
                sp.dma_start(out_v[b, :, :, :], out_sb[:]).then_inc(out_stored, 16)

            upto = Counts(sp)
            with sp.Fori(0, B - 1) as b:
                batch(b, True)
                upto.next_batch()
            batch(B - 1, False)
            sp.wait_ge(out_stored, 16 * B + 1)

        @block.gpsimd
        def _(pool):
            upto = Counts(pool)
            with pool.Fori(0, B) as b:
                for k in range(2):
                    pool.wait_ge(var_ready, upto(var_ready, k + 1))
                    nc.gpsimd.tensor_tensor(rstd[:], ve[:], half_sb[:], ALU.pow).then_inc(rstd_ready, 1)
                pool.wait_ge(gate_ready, upto(gate_ready, 1))
                for t in range(T):
                    pool.wait_ge(val_picked, upto(val_picked, (E - 1) * (t + 1)))
                    v_t = v_sb[:, t, :, 0:K]
                    g_t = gate[:, t * H:(t + 1) * H].unsqueeze(2).broadcast_to([128, H, K])
                    nc.gpsimd.tensor_tensor(v_t, v_t, g_t, ALU.mult).then_inc(val_ready, 1)
                for h in range(H):
                    if h:
                        pool.wait_ge(k_lo_ready, upto(k_lo_ready, h))
                    else:
                        pool.wait_ge(val_ready, upto(val_ready, T))
                    pool.wait_ge(k_hi_ready, upto(k_hi_ready, h + 1))
                    if h >= 2:
                        pool.wait_ge(score_ps, upto(score_ps, T * (h - 1)))
                    nc.gpsimd.tensor_tensor(k_l1[own(h), h % 2, :], qk[own(h), 1, h // 2, :],
                                            k_hh[own(h), h % 3, :].bitcast(f32), ALU.subtract).then_inc(k_lo_ready, 1)
                upto.next_batch()

        @block.scalar
        def _(act):
            act.wait_ge(small_loaded, 16 * SMALL_LOADS)
            nc.scalar.activation(sig_sb[:], cT_sb[:], ACT.Exp, scale=-1.0).then_inc(silu_exp_ready, 1)
            act.wait_ge(setup_ready, 1)
            upto = Counts(act)
            with act.Fori(0, B) as b:
                act.wait_ge(xnT_ps, upto(xnT_ps, 1))
                act.wait_ge(mod_picked, upto(mod_picked, 1))
                nc.scalar.activation(hT[:, 1:N + 1], bank(0, 2), ACT.Identity,
                                                      scale=modb[:, MOD_CA:MOD_CA + 1],
                                                      bias=modb[:, MOD_SA:MOD_SA + 1]).then_inc(hT_ready, 1)
                act.wait_ge(hT_ready, upto(hT_ready, 1))
                nc.scalar.activation(conv[:], hT[:, 1:N + 1], ACT.Identity,
                                                      scale=lw_sb[:, 1:2], bias=lb_sb[:]).then_inc(conv_mid, 1)
                act.wait_ge(kmin_ready, upto(kmin_ready, 1))
                nc.scalar.activation(ke, ke, ACT.Exp).then_inc(kexp_ready, 1)
                act.wait_ge(qmin_ready, upto(qmin_ready, 1))
                nc.scalar.activation(qe, qe, ACT.Exp).then_inc(qexp_ready, 1)
                act.wait_ge(xnT_ps, upto(xnT_ps, 2))
                act.wait_ge(out_stored, upto(out_stored, 0))
                nc.scalar.activation(h2T[:], bank(0, 2), ACT.Identity,
                                                       scale=modb[:, MOD_CB:MOD_CB + 1],
                                                       bias=modb[:, MOD_SB:MOD_SB + 1]).then_inc(h2T_ready, 1)
                act.wait_ge(top_ready, upto(top_ready, 1))
                nc.scalar.activation(gate[:], top[:], ACT.Exp, scale=-1.0).then_inc(topexp_ready, 1)
                for t in range(T):
                    act.wait_ge(proj_ps, upto(proj_ps, t + 1))
                    nc.scalar.activation(qk[:, t % 2, t // 2, :], bank(4 + 2 * (t % 2), 2),
                                         ACT.Copy).then_inc(proj_ready, 1)
                    act.wait_ge(val_ps, upto(val_ps, E * t + 1))
                    nc.scalar.activation(v_sb[:, t, :, 0:K], tiles(bank(E * t % 4), K), ACT.Copy).then_inc(val_first, 1)

                def upper_parts(h, step):
                    q, k = qk[own(h), 0, h // 2, :], qk[own(h), 1, h // 2, :]
                    if step == 0:
                        if h >= 3:
                            act.wait_ge(score_ps, upto(score_ps, T * (h - 2)))
                        nc.scalar.activation(q_hl[own(h), h % 3, :], q, ACT.Copy).then_inc(q_hi_ready, 1)
                    elif step == 1:
                        nc.scalar.activation(k_hh[own(h), h % 3, :], k, ACT.Copy).then_inc(k_hi_ready, 1)
                    else:
                        nc.scalar.activation(k_hh[other(h), h % 3, :], k, ACT.Copy).then_inc(k_hh_ready, 1)

                act.wait_ge(proj_ready, upto(proj_ready, 2 * HP))
                for h in range(2):
                    for step in range(3):
                        upper_parts(h, step)
                for h in range(H):
                    if h >= 2:
                        act.wait_ge(av_ps, upto(av_ps, 2 * (h - 1)))
                    for n, j in enumerate(KEY_ORDER):
                        act.wait_ge(score_ps, upto(score_ps, T * h + n + 1))
                        src = bank(3, 2)[:, 128 * j:N] if j < 4 else bank(5)[:, 128 * (j - 4):512]
                        nc.scalar.activation(p_sb[:, h % 2, P_AT[j]:P_AT[j + 1]], src, ACT.Exp,
                                             scale=SCALE).then_inc(prob_ready, 1)
                        if n in (1, 3, 5) and h + 2 < H:
                            upper_parts(h + 2, n // 2)
                act.wait_ge(selT_ps, upto(selT_ps, 1))
                nc.scalar.activation(selT[:], bank(6, 2)[0:H], ACT.Copy).then_inc(selT_ready, 1)
                for h in range(H):
                    act.wait_ge(oT_ps, upto(oT_ps, h // 2 + 1))
                    if h >= 4:
                        act.wait_ge(z_ready, upto(z_ready, EC * (h - 3)))
                    src = bank(2, 2)[K * (h % 2):K * (h % 2 + 1)]
                    nc.scalar.activation(oT[0:K, h % 4, :], src, ACT.Copy)
                    nc.scalar.activation(oT[K:2 * K, h % 4, :], src, ACT.Copy).then_inc(oT_ready, 1)
                act.wait_ge(z_used, upto(z_used, H * EC))
                nc.scalar.activation(yT[:], bank(0, 2), ACT.Copy,
                                                      scale=modb[:, MOD_GB:MOD_GB + 1]).then_inc(yT_ready, 1)
                upto.next_batch()

        @block.vector
        def _(dve):
            v = nc.vector

            steps = [0]
            for ahead in one_ahead.values():
                dve.sem_inc(ahead, 1)

            def link0(ins):
                steps[0] += 1
                ins.then_inc(dve_step, 1)
                dve.wait_ge(dve_step, steps[0])

            v.memset(hT[:, 0:1], 0.0)
            v.memset(hT[:, N + 1:N + 2], 0.0)
            v.memset(q_hm[:].bitcast(f32), 0.0)
            v.memset(k_l1[:].bitcast(f32), 0.0).then_inc(dve_step, 1)
            steps[0] += 1
            dve.wait_ge(dve_step, steps[0])
            for h in range(2):
                v.memset(k_l1[other(h).start:other(h).start + 1, h, :].bitcast(f32), 1.0)
            v.memset(ones_sb[:], 1.0)
            v.memset(half_sb[:], -0.5)
            dve.wait_ge(small_loaded, 16 * SMALL_LOADS)
            v.tensor_copy(ident_b[:], ident)
            v.tensor_copy(causal_b[:], const("causal"))
            v.tensor_copy(causal_tb[:], const("causal_t"))
            v.tensor_copy(row_of_b[:], const("row_of", H))
            v.tensor_scalar(bq1_sb[:], bq_sb[:], 1.0, None, ALU.add)
            dve.wait_ge(silu_exp_ready, 1)
            link0(v.tensor_scalar(sig_sb[:], sig_sb[:], 1.0, None, ALU.add))
            link0(v.reciprocal(sig_sb[:], sig_sb[:]))
            v.tensor_tensor(silu_sb[:], sig_sb[:], cT_sb[:], ALU.mult).then_inc(silu_ready, 1)
            dve.wait_ge(mod_ps_ready, 1)
            link0(v.tensor_copy(mod_sb[:].rearrange("p m b -> p (m b)"), bank(0)[:, 0:6 * B]))
            for m in (MOD_CA, MOD_CB):
                link0(v.tensor_scalar(mod_sb[:, m, :], mod_sb[:, m, :], 1.0, None, ALU.add))
            link0(v.tensor_copy(ga_row[:].rearrange("p b c -> p (b c)"), bank(1)))

            def clamp(ap, sign):
                link0(v.tensor_scalar(sign, ap, 0.0, 2.0, ALU.is_ge, ALU.mult))
                link0(v.tensor_scalar(sign, sign, -1.0, None, ALU.add))
                link0(v.tensor_tensor(ap, ap, sign, ALU.mult))
                link0(v.tensor_scalar(ap, ap, 0.25, None, ALU.max))
                link0(v.tensor_tensor(ap, ap, sign, ALU.mult))

            clamp(mod_sb[:, MOD_GB, :], sign_sb[:, 0:B])
            clamp(ga_row[:].rearrange("p b c -> p (b c)"), sign_sb[:])
            v.memset(ve[:], 1.0).then_inc(setup_ready, 1)
            dve.wait_ge(setup_ready, 1)
            base = steps[0]

            upto = Counts(dve)
            with dve.Fori(0, B) as b:
                links = [0]

                def link(ins):
                    links[0] += 1
                    ins.then_inc(dve_step, 1)
                    dve.wait_ge(dve_step, upto(dve_step, base + links[0]))

                def normalise(src, k):
                    for t in range(T):
                        last = v.bn_stats(stats[:, t, :], src[:, t, :])
                    link(last)
                    dve.sem_inc(wait_carried, 1)
                    for t in range(T):
                        last = v.bn_aggr(mv[:, t, :], stats[:, t, :])
                    link(last)
                    v.tensor_scalar(ve[:], mv[:, :, 1], EPS, None, ALU.add).then_inc(var_ready, 1)
                    dve.wait_ge(rstd_ready, upto(rstd_ready, k + 1))
                    for t in range(T):
                        v.tensor_scalar(xn[:, t, :], src[:, t, :], mv[:, t, 0:1], rstd[:, t:t + 1],
                                                         ALU.subtract, ALU.mult).then_inc(xn_ready, 1)

                dve.wait_ge(yT_ready, upto(yT_ready, 0))
                v.tensor_copy(modb[:], mod_sb[:, :, bass.ds(b, 1)].rearrange("p m b -> p (m b)")).then_inc(mod_picked, 1)
                dve.wait_ge(x_loaded, upto(x_loaded, 16))
                normalise(x_sb, 0)

                dve.wait_ge(hn_ps, upto(hn_ps, 1))
                v.tensor_copy(hn[:, :, 0:C], tiles(bank(2, 2)))
                v.memset(hn[:, :, C:C + 1], 1.0).then_inc(hn_ready, 1)
                dve.wait_ge(k_ps, upto(k_ps, 1))
                v.tensor_scalar(ke, bank(6, 2), 0.0, None, ALU.min).then_inc(kmin_ready, 1)
                dve.wait_ge(q_ps, upto(q_ps, 1))
                v.tensor_scalar(qe, bank(4, 2), bq_sb[:], 0.0, ALU.add, ALU.min).then_inc(qmin_ready, 1)
                dve.wait_ge(kexp_ready, upto(kexp_ready, 1))
                v.scalar_tensor_tensor(kn, bank(6, 2), 1.0, ke, ALU.add, ALU.max).then_inc(k_ready, 1)
                dve.wait_ge(qexp_ready, upto(qexp_ready, 1))
                v.scalar_tensor_tensor(qT, bank(4, 2), bq1_sb[:], qe, ALU.add, ALU.max).then_inc(qT_ready, 1)
                dve.wait_ge(kv_ps, upto(kv_ps, 1))
                v.tensor_tensor(kv_sb[:], bank(0)[:, 0:C], const("same_head"), ALU.mult).then_inc(kv_ready, 1)
                link(v.tensor_copy(ksum[:], bank(0)[:, C:C + 1]))
                v.tensor_scalar(kvz[:, C:C + LH], const("head_of"), ksum[:], None, ALU.mult).then_inc(kmean_ready, 1)
                dve.wait_ge(rkv_ps, upto(rkv_ps, 1))
                v.tensor_copy(rkv_sb[:], bank(1)[:, 0:C]).then_inc(rkv_ready, 1)
                dve.wait_ge(rrkv_ps, upto(rrkv_ps, 1))
                v.tensor_copy(kvz[:, 0:C], bank(0)[:, 0:C]).then_inc(rrkv_ready, 1)
                dve.wait_ge(conv_mid, upto(conv_mid, 1))
                link(v.scalar_tensor_tensor(conv[:], hT[:, 0:N], lw_sb[:, 0:1], conv[:], ALU.mult, ALU.add))
                v.scalar_tensor_tensor(conv[:], hT[:, 2:N + 2], lw_sb[:, 2:3], conv[:],
                                                          ALU.mult, ALU.add).then_inc(conv_ready, 1)
                dve.wait_ge(att_ps, upto(att_ps, 1))
                link(v.tensor_scalar(den[:], bank(4)[:, 0:T * LH], 1e-6, None, ALU.add))
                link(v.reciprocal(den[:], den[:]))
                att_h = att[:].rearrange("p t (h d) -> p (t h) d", d=LD)
                link(v.tensor_tensor(att_h, tiles(bank(2, 2), LD), den[:].unsqueeze(2).broadcast_to([128, T * LH, LD]),
                                     ALU.mult))
                dve.wait_ge(conv_ps, upto(conv_ps, 1))
                link(v.tensor_tensor(att[:], att[:], tiles(bank(6, 2)), ALU.add))
                link(v.tensor_tensor(att[:], att[:], ga_row[:, bass.ds(b, 1), :].broadcast_to([128, T, C]), ALU.mult))
                v.tensor_tensor(x1_sb[:], att[:], x_sb[:], ALU.add).then_inc(x1_ready, 1)
                dve.wait_ge(x1_ready, upto(x1_ready, 1))
                normalise(x1_sb, 1)

                dve.wait_ge(logit_ps, upto(logit_ps, 1))
                link(v.tensor_scalar(lg[:], tiles(bank(2), E), SATURATED, None, ALU.min))
                v.tensor_reduce(top[:], lg[:], AX.X, ALU.max).then_inc(top_ready, 1)
                dve.wait_ge(top_ready, upto(top_ready, 1))
                link(v.tensor_tensor(eq[:], lg[:], top[:].unsqueeze(2).broadcast_to([128, T * H, E]), ALU.is_equal))
                link(v.tensor_tensor(eq[:], eq[:], const("rank").unsqueeze(1).broadcast_to([128, T * H, E]), ALU.mult))
                link(v.tensor_reduce(best[:], eq[:], AX.X, ALU.max))
                v.tensor_scalar(sel[:], best[:], -1.0, float(E), ALU.mult, ALU.add)
                link(v.tensor_tensor(mask[:], eq[:], best[:].unsqueeze(2).broadcast_to([128, T * H, E]), ALU.is_equal))
                dve.wait_ge(topexp_ready, upto(topexp_ready, 1))
                link(v.tensor_scalar(gate[:], gate[:], 1.0, None, ALU.add))
                v.reciprocal(gate[:], gate[:]).then_inc(gate_ready, 1)

                for t in range(T):
                    dve.wait_ge(val_first, upto(val_first, t + 1))
                    for e in range(1, E):
                        dve.wait_ge(val_ps, upto(val_ps, E * t + e + 1))
                        dve.sem_inc(wait_carried, 1)
                        pick = mask[:, t * H:(t + 1) * H, e:e + 1].bitcast(u32).broadcast_to([128, H, K])
                        v.copy_predicated(v_sb[:, t, :, 0:K], pick, tiles(bank((E * t + e) % 4), K)).then_inc(val_picked, 1)
                        dve.wait_ge(val_picked, upto(val_picked, (E - 1) * t + e))
                S_ones = v.memset(v_sb[:, :, :, K:K + 1], 1.0)
                S_ones.then_inc(mask_ready, 1)

                def maxima(h, ns):
                    for n in ns:
                        t = MAX_ORDER[n]
                        dve.wait_ge(max_ps, upto(max_ps, T * h + n + 1))
                        src = bank(1, 2)[:, 0:128 * (t + 1)] if t >= 4 else bank(0)[:, 0:128 * (t + 1)]
                        v.tensor_reduce(m8[:, h % 2, t:t + 1], src, AX.X, ALU.max).then_inc(max_ready, 1)

                def max_row(h):
                    dve.wait_ge(maxrow_ps, upto(maxrow_ps, h + 1))
                    if h >= 2:
                        dve.wait_ge(maxrow_in, upto(maxrow_in, 16 * (h - 1)))
                    v.tensor_scalar(mrow[:, h % 2, :], bank(0)[0:T, 0:128], -1.0, None,
                                                         ALU.mult).then_inc(maxrow_ready, 1)

                def lower_queries(h):
                    dve.wait_ge(q_hi_ready, upto(q_hi_ready, h + 1))
                    v.tensor_tensor(q_hl[other(h), h % 3, :], qk[own(h), 0, h // 2, :],
                                    q_hl[own(h), h % 3, :].bitcast(f32), ALU.subtract).then_inc(q_lo_ready, 1)

                def upper_queries(h):
                    if h >= 2:
                        dve.wait_ge(score_ps, upto(score_ps, T * (h - 1)))
                    v.tensor_copy(q_hm[own(h), h % 2, :], q_hl[own(h), h % 3, :].bitcast(f32)).then_inc(q_hm_ready, 1)

                def heads_out(h, half):
                    dve.wait_ge(av_ps, upto(av_ps, 2 * h + half + 1))
                    src = bank(6 + half)[:, 0:4 * (K + 1)].rearrange("p (t k) -> p t k", k=K + 1)
                    link(v.reciprocal(rden[:, half, :], src[:, :, K]))
                    g = gate[:].rearrange("p (t h) -> p t h", h=H)[:, 4 * half:4 * half + 4, h]
                    link(v.tensor_tensor(rden[:, half, :], rden[:, half, :], g, ALU.mult))
                    v.tensor_tensor(o_sb[:, 4 * half:4 * half + 4, h, :], src[:, :, 0:K],
                                                    rden[:, half, :].unsqueeze(2).broadcast_to([128, 4, K]), ALU.mult).then_inc(o_ready, 1)

                lower_queries(0)
                upper_queries(0)
                maxima(0, range(T))
                lower_queries(1)
                max_row(0)
                for h in range(H + 1):
                    if h + 1 < H:
                        maxima(h + 1, range(4))
                        upper_queries(h + 1)
                        maxima(h + 1, (4, 5))
                    if h >= 1:
                        heads_out(h - 1, 0)
                    if h + 1 < H:
                        maxima(h + 1, (6, 7))
                        max_row(h + 1)
                    if h + 2 < H:
                        lower_queries(h + 2)
                    if h >= 1:
                        heads_out(h - 1, 1)

                for h in range(H):
                    dve.wait_ge(oT_ready, upto(oT_ready, h + 1))
                    dve.wait_ge(selB_ps, upto(selB_ps, h + 1))
                    for c in range(EC):
                        n = EC * h + c
                        if n >= 4:
                            dve.wait_ge(z_used, upto(z_used, n - 3))
                        v.scalar_tensor_tensor(z[:, n % 4, :], bank(4 + 2 * (h % 2), 2),
                                                               const("expert_of")[:, c:c + 1], oT[:, h % 4, :],
                                                               ALU.is_equal, ALU.mult).then_inc(z_ready, 1)
                dve.wait_ge(y_ps, upto(y_ps, 1))
                dve.wait_ge(out_stored, upto(out_stored, 0))
                v.tensor_tensor(out_sb[:], x1_sb[:], tiles(bank(2, 2)), ALU.add).then_inc(out_ready, 1)
                assert links[0] == DVE_STEPS, links[0]
                upto.next_batch()

        @block.tensor
        def _(pe):
            mm = nc.tensor.matmul
            pe.wait_ge(silu_ready, 1)
            for m in range(6):
                mm(bank(0)[:, m * B:(m + 1) * B], wmod_view(m), silu_sb[:], start=True, stop=True)
            for i in range(B):
                last = mm(bank(1)[:, i * C:(i + 1) * C], silu_sb[:, i:i + 1].broadcast_to([C, 128]), wmod_view(MOD_GA),
                          start=True, stop=True)
            last.then_inc(mod_ps_ready, 1)
            pe.wait_ge(setup_ready, 1)

            upto = Counts(pe)
            with pe.Fori(0, B) as b:
                def transpose_tiles(first, src, signal, width=128, waits=None):
                    for t in range(T):
                        if waits:
                            waits(t)
                        last = nc.tensor.transpose(bank(first, 2)[0:width, t * 128:(t + 1) * 128], src(t), ident)
                    last.then_inc(signal, 1)

                pe.wait_ge(yT_ready, upto(yT_ready, 0))
                pe.wait_ge(out_ready, upto(out_ready, 0))
                pe.wait_ge(z_ready, upto(z_ready, 0))
                transpose_tiles(0, lambda t: xn[:, t, :], xnT_ps, waits=lambda t: pe.wait_ge(xn_ready, upto(xn_ready, t + 1)))
                pe.wait_ge(hT_ready, upto(hT_ready, 1))
                transpose_tiles(2, lambda t: hT[:, 1 + t * 128:1 + (t + 1) * 128], hn_ps)
                for i in range(2):
                    mm(bank(6 + i), ones_sb[:], bk_sb[:].unsqueeze(1).broadcast_to([1, 4, C]), start=True, stop=True)
                    for t in range(4):
                        n = 4 * i + t
                        last = mm(bank(6 + i)[:, t * C:(t + 1) * C], hT[:, 1 + n * 128:1 + (n + 1) * 128],
                                  wqk_sb[:, C:2 * C], start=False, stop=True, skip_group_check=True)
                last.then_inc(k_ps, 1)
                for i in range(2):
                    last = mm(bank(4 + i), wqk_sb[:, 0:C], hT[:, 1 + i * 512:1 + (i + 1) * 512], start=True, stop=True)
                last.then_inc(q_ps, 1)
                pe.wait_ge(hn_ready, upto(hn_ready, 1))
                pe.wait_ge(k_ready, upto(k_ready, 1))
                for t in range(T):
                    last = mm(bank(0)[:, 0:C + 1], kn[:, t * C:(t + 1) * C], hn[:, t, :], start=t == 0, stop=t == T - 1)
                last.then_inc(kv_ps, 1)
                pe.wait_ge(kv_ready, upto(kv_ready, 1))
                mm(bank(1)[:, 0:C], const("rot_t"), kv_sb[:], start=True, stop=True).then_inc(rkv_ps, 1)
                pe.wait_ge(rkv_ready, upto(rkv_ready, 1))
                pe.wait_ge(kmean_ready, upto(kmean_ready, 1))
                mm(bank(0)[:, 0:C], const("rot"), rkv_sb[:], start=True, stop=True).then_inc(rrkv_ps, 1)
                pe.wait_ge(rrkv_ready, upto(rrkv_ready, 1))
                pe.wait_ge(qT_ready, upto(qT_ready, 1))
                for t in range(T):
                    mm(bank(2, 2)[:, t * C:(t + 1) * C], qT[:, t * 128:(t + 1) * 128], kvz[:, 0:C],
                       start=True, stop=True)
                    last = mm(bank(4)[:, t * LH:(t + 1) * LH], qT[:, t * 128:(t + 1) * 128], kvz[:, C:C + LH],
                              start=True, stop=True)
                last.then_inc(att_ps, 1)
                pe.wait_ge(conv_ready, upto(conv_ready, 1))
                transpose_tiles(6, lambda t: conv[:, t * 128:(t + 1) * 128], conv_ps)
                transpose_tiles(0, lambda t: xn[:, t, :], xnT_ps,
                                waits=lambda t: pe.wait_ge(xn_ready, upto(xn_ready, T + t + 1)))

                pe.wait_ge(proj_loaded, 16 * 4)
                pe.wait_ge(h2T_ready, upto(h2T_ready, 1))
                for t in range(T):
                    last = mm(bank(2)[:, t * H * E:(t + 1) * H * E], h2T[:, t * 128:(t + 1) * 128], wg_sb[:],
                              start=True, stop=True)
                last.then_inc(logit_ps, 1)
                for t in range(T):
                    if t >= 2:
                        pe.wait_ge(proj_ready, upto(proj_ready, t - 1))
                    w = (wq_sb, wk_sb)[t % 2][:, t // 2 * 128:(t // 2 + 1) * 128]
                    for i in range(2):
                        last = mm(bank(4 + 2 * (t % 2) + i), w, h2T[:, i * 512:(i + 1) * 512], start=True, stop=True)
                    last.then_inc(proj_ps, 1)
                    for e in range(E):
                        n = E * t + e
                        if n == 2:
                            pe.wait_ge(top_ready, upto(top_ready, 1))
                        if n >= 4:
                            t4, e4 = divmod(n - 4, E)
                            if e4:
                                pe.wait_ge(val_picked, upto(val_picked, (E - 1) * t4 + e4))
                            else:
                                pe.wait_ge(val_first, upto(val_first, t4 + 1))
                        mm(bank(n % 4), h2T[:, t * 128:(t + 1) * 128], v_w[:, e, :],
                                          start=True, stop=True).then_inc(val_ps, 1)

                def max_tile(h, n):
                    t = MAX_ORDER[n]
                    if n >= 2:
                        pe.wait_ge(max_ready, upto(max_ready, T * h + n - 1))
                    elif h:
                        pe.wait_ge(max_ready, upto(max_ready, T * h))
                        pe.wait_ge(maxrow_ready, upto(maxrow_ready, h))
                    dst = bank(1, 2) if t >= 4 else bank(0)
                    if n == 0:
                        pe.wait_ge(q_lo_ready, upto(q_lo_ready, h + 1))
                        pe.wait_ge(k_hh_ready, upto(k_hh_ready, h + 1))
                    q = q_hl[:, h % 3, t * 128:(t + 1) * 128]
                    w = 128 * (t + 1)
                    for at in range(0, w, 512):
                        to = min(at + 512, w)
                        mm(dst[:, at:to], q, k_hh[:, h % 3, at:to], start=True, stop=True)
                    mm(dst[:, w - 128:w], ident_b[:], causal_b[:], start=False, stop=True,
                                       skip_group_check=True).then_inc(max_ps, 1)

                def max_row(h):
                    pe.wait_ge(max_ready, upto(max_ready, T * (h + 1)))
                    nc.tensor.transpose(bank(0)[0:T, 0:128], m8[:, h % 2, :], ident).then_inc(maxrow_ps, 1)

                def score_tile(h, n):
                    j = KEY_ORDER[n]
                    if n >= 2:
                        pe.wait_ge(prob_ready, upto(prob_ready, T * h + n - 1))
                    else:
                        if h:
                            pe.wait_ge(prob_ready, upto(prob_ready, T * h))
                        pe.wait_ge(maxrow_in, upto(maxrow_in, 16 * (h + 1)))
                    dst, off = (bank(3, 2), 0) if j < 4 else (bank(5), 512)
                    if n == 0:
                        pe.wait_ge(q_hm_ready, upto(q_hm_ready, h + 1))
                        pe.wait_ge(k_lo_ready, upto(k_lo_ready, h + 1))
                    edge = max(512, 128 * (j + 1)) if j < 4 else N
                    spans = [(at, to) for at, to in ((128 * j, edge), (edge, N)) if at < to]
                    for k, q, start in ((k_hh[:, h % 3], q_hl[:, h % 3], True), (k_l1[:, h % 2], q_hm[:, h % 2], False)):
                        for at, to in spans:
                            last = mm(dst[:, at - off:to - off], k[:, j * 128:(j + 1) * 128], q[:, at:to], start=start,
                                      stop=True, skip_group_check=not start)
                    at = 128 * j
                    return mm(dst[:, at - off:at - off + 128], ident_b[:], causal_tb[:], start=False, stop=True,
                              skip_group_check=True)

                def av_tile(h, i):
                    need = 1 + max(KEY_ORDER.index(j) for j in range(i + 1))
                    pe.wait_ge(prob_ready, upto(prob_ready, T * h + need))
                    half = i // 4
                    if i % 4 == 0 and h:
                        pe.wait_ge(o_ready, upto(o_ready, 2 * (h - 1) + half + 1))
                    for j in range(i + 1):
                        at = P_AT[j] + 128 * (i - j)
                        last = mm(bank(6 + half)[:, (i % 4) * (K + 1):(i % 4 + 1) * (K + 1)],
                                  p_sb[:, h % 2, at:at + 128], v_sb[:, j, h, :], start=j == 0, stop=j == i)
                    if i % 4 == 3:
                        last.then_inc(av_ps, 1)

                pe.wait_ge(val_picked, upto(val_picked, T * (E - 1)))
                pe.wait_ge(val_first, upto(val_first, T))
                pe.wait_ge(proj_ready, upto(proj_ready, 2 * HP))
                for n in range(T):
                    max_tile(0, n)
                max_row(0)
                for h in range(H + 1):
                    if h == 1:
                        pe.wait_ge(val_ready, upto(val_ready, T))
                        pe.wait_ge(mask_ready, upto(mask_ready, 1))
                    for what, n in HEAD_ORDER:
                        if what == "max" and h + 1 < H:
                            max_tile(h + 1, n)
                        if what == "row" and h + 1 < H:
                            max_row(h + 1)
                        if what == "score" and h < H:
                            score_tile(h, n).then_inc(score_ps, 1)
                        if what == "values" and h >= 1:
                            av_tile(h - 1, n)

                pe.wait_ge(o_ready, upto(o_ready, 2 * H))
                transpose_tiles(6, lambda t: sel[:, t * H:(t + 1) * H], selT_ps, width=H)
                pe.wait_ge(selT_ready, upto(selT_ready, 1))

                def spread(h):
                    if h % 2 == 0:
                        if h:
                            pe.wait_ge(oT_ready, upto(oT_ready, h))
                        transpose_tiles(2, lambda t: o_sb[:, t, h:h + 2, :].rearrange("p h k -> p (h k)"), oT_ps)
                    if h >= 2:
                        pe.wait_ge(z_ready, upto(z_ready, EC * (h - 1)))
                    for i in range(2):
                        last = mm(bank(4 + 2 * (h % 2) + i), row_of_b[:, h * 128:(h + 1) * 128],
                                  selT[:, i * 512:(i + 1) * 512], start=True, stop=True)
                    last.then_inc(selB_ps, 1)

                spread(0)
                for h in range(H):
                    if h + 1 < H:
                        spread(h + 1)
                    for c in range(EC):
                        n = EC * h + c
                        pe.wait_ge(z_ready, upto(z_ready, n + 1))
                        for i in range(2):
                            last = mm(bank(i), o_w[:, n, :], z[:, n % 4, i * 512:(i + 1) * 512],
                                      start=n == 0, stop=n == H * EC - 1)
                        last.then_inc(z_used, 1)
                pe.wait_ge(yT_ready, upto(yT_ready, 1))
                transpose_tiles(2, lambda t: yT[:, t * 128:(t + 1) * 128], y_ps)
                upto.next_batch()


def constants():
    p = np.arange(128)
    theta = (np.float32(1.0) / np.float32(10000.0) ** (np.arange(C // 2, dtype=np.float32) / np.float32(C // 2)))
    cos, sin = np.cos(theta.astype(np.float32)), np.sin(theta.astype(np.float32))
    rot = np.zeros((C, C), np.float32)
    even = 2 * np.arange(C // 2)
    rot[even, even], rot[even, even + 1], rot[even + 1, even], rot[even + 1, even + 1] = cos, -sin, sin, cos
    parts = {
        "ident": np.eye(128),
        "rot": rot, "rot_t": rot.T,
        "same_head": (p[:, None] // LD == p[None, :] // LD) / N,
        "head_of": (p[:, None] // LD == np.arange(LH)[None, :]) / N,
        "rank": np.broadcast_to(E - np.arange(E), (128, E)),
        "expert_of": 2 * np.arange(EC)[None, :] + p[:, None] // K,
        "causal": np.where(p[None, :] > p[:, None], MASKED, 0.0),
        "causal_t": np.where(p[:, None] > p[None, :], MASKED, 0.0),
        "row_of": (p[:, None] == np.arange(H * 128)[None, :] // 128),
    }
    return np.concatenate([np.asarray(parts[n], np.float32) for n in CONSTS], axis=1)


def kernel(L0_attn_x, L0_attn_W_qk, L0_attn_b_qk, L0_attn_lepe_w, L0_attn_lepe_b, L0_ffn_w_q, L0_ffn_w_k,
           L0_ffn_w_gate, L0_ffn_value_experts, L0_ffn_output_experts, L0_c, L0_wmod):
    import concourse.bacc as bacc
    from concourse.bass_utils import run_bass_kernel_spmd

    b_qk = np.asarray(L0_attn_b_qk)
    arrays = dict(
        x=L0_attn_x,
        w_qk_t=np.asarray(L0_attn_W_qk).T,
        b_q=b_qk[:C].reshape(C, 1), b_k=b_qk[C:].reshape(1, C),
        lepe_w=np.asarray(L0_attn_lepe_w).reshape(C, 3), lepe_b=np.asarray(L0_attn_lepe_b).reshape(C, 1),
        w_q=L0_ffn_w_q, w_k=L0_ffn_w_k, w_gate=L0_ffn_w_gate,
        v_exp=np.asarray(L0_ffn_value_experts).transpose(2, 0, 1, 3).reshape(C, E, H * K),
        o_exp=np.asarray(L0_ffn_output_experts).reshape(EC, 2, H, K, C).transpose(1, 3, 2, 0, 4).reshape(
            128, H * EC, C),
        c_t=np.asarray(L0_c).T, w_mod=L0_wmod, consts=constants(),
    )
    arrays = {n: np.ascontiguousarray(a) for n, a in arrays.items()}
    nc = bacc.Bacc("TRN2", target_bir_lowering=False, num_devices=1)
    aps = {n: nc.dram_tensor(n, a.shape, mybir.dt.from_np(a.dtype), kind="ExternalInput").ap()
           for n, a in arrays.items()}
    out = nc.dram_tensor("out", (B, N, C), mybir.dt.float32, kind="ExternalOutput").ap()
    adaln_block(nc, out=out, **aps)
    return run_bass_kernel_spmd(nc, [arrays], core_ids=[0]).results[0]["out"]
```

```python
from contextlib import ExitStack

import numpy as np

import concourse.bass as bass
from concourse import mybir

B, N, C = 4, 1024, 128
T = N // 128
LH = 16
LD = C // LH
H, K, E = 8, 64, 8
HP = H // 2
EC = E * K // 128
SCALE = float(K) ** -0.5
EPS = 1e-5
MASKED = -1e30
SATURATED = 17.0
MOD_SA, MOD_CA, MOD_GA, MOD_SB, MOD_CB, MOD_GB = range(6)

CONSTS = {"ident": C, "rot": C, "rot_t": C, "same_head": C, "head_of": LH, "rank": E, "expert_of": EC,
          "causal": 128, "causal_t": 128, "row_of": H * 128}
KEPT = 7
CONST_AT = {n: sum(list(CONSTS.values())[:i]) for i, n in enumerate(CONSTS)}

MAX_ORDER = [4, 0, 5, 1, 6, 2, 7, 3]
KEY_ORDER = [0, 4, 1, 5, 2, 6, 3, 7]
HEAD_ORDER = (
    ("max", (0, 1)), ("values", (0, 1, 2)), ("score", (0,)), ("max", (2, 3)), ("score", (1,)), ("values", (3,)),
    ("score", (2, 3)), ("max", (4, 5)), ("values", (4,)), ("score", (4, 5)), ("max", (6, 7)), ("values", (5,)),
    ("score", (6, 7)), ("row", ()), ("values", (6, 7)),
)
FIRST_ORDER = (
    ("score", (0,)), ("score", (1,)), ("max", (0, 1)), ("score", (2,)), ("max", (2, 3)), ("score", (3,)),
    ("max", (4, 5)), ("score", (4, 5)), ("max", (6, 7)), ("score", (6, 7)),
)
VALUE_ORDER = [(t + i, e) for t in range(0, T, 2) for e in range(E) for i in range(2)]
PICKS = [sum(e > 0 for _, e in VALUE_ORDER[:n]) for n in range(T * E + 1)]
PROJECTED = {2: 2, 5: 3, 8: 4, 14: 5, 22: 6, 30: 7}
VALUES_MAX = {10 + 3 * i: divmod(i, T) for i in range(2 * T)}
VALUES_ROW = {10 + 3 * (T - 1) + 2: 0, 10 + 3 * (2 * T - 1) + 2: 1}
P_AT = [128 * (T * j - j * (j - 1) // 2) for j in range(T + 1)]

SMALL_LOADS = 10
DVE_STEPS = 49


def adaln_block(nc, x, w_qk_t, b_q, b_k, lepe_w, lepe_b, w_q, w_k, w_gate, v_exp, o_exp, c_t, w_mod, consts, out):
    f32, bf16, u32, f32r = mybir.dt.float32, mybir.dt.bfloat16, mybir.dt.uint32, mybir.dt.float32r
    ALU, ACT, AX = mybir.AluOpType, mybir.ActivationFunctionType, mybir.AxisListType

    ctx = ExitStack()
    with ctx:
        def sb(name, shape, dt=f32):
            return ctx.enter_context(nc.sbuf_tensor(name, shape, dt))

        def in_one_place(name, shape, dt, name_2, shape_2, dt_2):
            at = -(-nc.sbuf_base // 32) * 32
            second = sb(name_2, shape_2, dt_2)
            return nc.alloc_sbuf_tensor_at(name, shape, dt, offset=at), second

        per_batch = {}

        def sem(name, per=0):
            made = ctx.enter_context(nc.semaphore(name))
            per_batch[id(made)] = per
            return made

        def own(h):
            return slice(K * (h % 2), K * (h % 2) + K)

        def other(h):
            return own(h + 1)

        def tiles(ap, w=C):
            return ap.rearrange("p (t c) -> p t c", c=w)

        small_loaded = sem("small_loaded")
        proj_loaded = sem("proj_loaded")
        silu_exp_ready = sem("silu_exp_ready")
        silu_ready = sem("silu_ready")
        mod_ps_ready = sem("mod_ps_ready")
        v_hi_ready = sem("v_hi_ready")
        w_hi_ready = sem("w_hi_ready")
        w_lo_ready = sem("w_lo_ready")
        wait_carried = sem("wait_carried")
        x_loaded = sem("x_loaded", 16)
        mod_picked = sem("mod_picked", 1)
        var_ready = sem("var_ready", 2)
        rstd_ready = sem("rstd_ready", 2)
        xn_ready = sem("xn_ready", 2 * T)
        xnT_ps = sem("xnT_ps", 2)
        hT_ready = sem("hT_ready", 1)
        h2T_ready = sem("h2T_ready", 1)
        h2_hi_ready = sem("h2_hi_ready", 1)
        h2_lo_ready = sem("h2_lo_ready", 1)
        v_loaded_again = sem("v_loaded_again", 16)
        v_lo_ready = sem("v_lo_ready", E)
        hn_ps = sem("hn_ps", 1)
        hn_ready = sem("hn_ready", 1)
        q_ps = sem("q_ps", 1)
        k_ps = sem("k_ps", 1)
        qneg_ready = sem("qneg_ready", 1)
        kneg_ready = sem("kneg_ready", 1)
        qexp_ready = sem("qexp_ready", 1)
        kexp_ready = sem("kexp_ready", 1)
        qT_ready = sem("qT_ready", 1)
        k_ready = sem("k_ready", 1)
        conv_mid = sem("conv_mid", 1)
        conv_ready = sem("conv_ready", 1)
        kv_ps = sem("kv_ps", 1)
        kv_ready = sem("kv_ready", 1)
        kmean_ready = sem("kmean_ready", 1)
        rkv_ps = sem("rkv_ps", 1)
        rkv_ready = sem("rkv_ready", 1)
        rrkv_ps = sem("rrkv_ps", 1)
        rrkv_ready = sem("rrkv_ready", 1)
        att_ps = sem("att_ps", 1)
        den_ps = sem("den_ps", 1)
        den_ready = sem("den_ready", 1)
        att_ready = sem("att_ready", 1)
        conv_ps = sem("conv_ps", 1)
        x1_ready = sem("x1_ready", 1)
        x1_kept = sem("x1_kept", 1)
        logit_ps = sem("logit_ps", 1)
        top_ready = sem("top_ready", 1)
        topexp_ready = sem("topexp_ready", 1)
        gate_ready = sem("gate_ready", 1)
        mask_ready = sem("mask_ready", 1)
        proj_ps = sem("proj_ps", 2 * HP)
        proj_ready = sem("proj_ready", 2 * HP)
        val_ps = sem("val_ps", T * E)
        val_first = sem("val_first", T)
        val_picked = sem("val_picked", T * (E - 1))
        val_ready = sem("val_ready", T)
        max_ps = sem("max_ps", T * H)
        max_ready = sem("max_ready", T * H)
        maxrow_ps = sem("maxrow_ps", H)
        maxrow_ready = sem("maxrow_ready", H)
        maxrow_in = sem("maxrow_in", 16 * H)
        q_hi_ready = sem("q_hi_ready", H)
        k_hi_ready = sem("k_hi_ready", H)
        k_hh_ready = sem("k_hh_ready", H)
        q_lo_ready = sem("q_lo_ready", H)
        q_hm_ready = sem("q_hm_ready", H)
        k_lo_ready = sem("k_lo_ready", H)
        score_ps = sem("score_ps", T * H)
        prob_ready = sem("prob_ready", T * H)
        av_ps = sem("av_ps", 2 * H)
        o_ready = sem("o_ready", 2 * H)
        gb_ready = sem("gb_ready", 1)
        selT_ps = sem("selT_ps", 1)
        selT_ready = sem("selT_ready", 1)
        oT_ps = sem("oT_ps", HP)
        oT_ready = sem("oT_ready", H)
        selB_ps = sem("selB_ps", H)
        z_ready = sem("z_ready", H * EC)
        z_used = sem("z_used", H * EC)
        yT_ready = sem("yT_ready", 1)
        y_ps = sem("y_ps", 1)
        out_ready = sem("out_ready", 1)
        out_stored = sem("out_stored", 16)
        dve_step = sem("dve_step", DVE_STEPS)
        one_ahead = {"yT_ready": yT_ready, "out_ready": out_ready, "out_stored": out_stored}

        kept = sum(list(CONSTS.values())[:KEPT])
        cst = sb("cst", [128, kept])

        def const(name, rows=128):
            at, tensor = CONST_AT[name], cst
            if at >= kept:
                at, tensor = at - kept, cst_once
            return tensor[0:rows, at:at + CONSTS[name]]

        ident = const("ident")
        wqk_sb = sb("wqk_sb", [C, 2 * C])
        bq_sb, bk_sb = sb("bq_sb", [C, 1]), sb("bk_sb", [1, C])
        bq1_sb, bqm_sb = sb("bq1_sb", [C, 1]), sb("bqm_sb", [C, 1])
        lw_sb, lb_sb = sb("lw_sb", [C, 3]), sb("lb_sb", [C, 1])
        w_hi, w_lo = sb("w_hi", [C, 2, H * K], f32r), sb("w_lo", [C, 2, H * K], f32r)
        wg_sb = sb("wg_sb", [C, H * E])
        v_hi = sb("v_hi", [C, E, H * K], f32r)
        o_w = sb("o_w", [128, H * EC, C])
        cT_sb, sig_sb, silu_sb = sb("cT_sb", [C, B]), sb("sig_sb", [C, B]), sb("silu_sb", [C, B])
        mod_sb = sb("mod_sb", [C, 6, B])
        ga_row = sb("ga_row", [128, B, C])
        ident_b = sb("ident_b", [128, 128], bf16)
        causal_b, causal_tb = sb("causal_b", [128, 128], bf16), sb("causal_tb", [128, 128], bf16)
        row_of_b = sb("row_of_b", [H, H * 128], bf16)
        ones_sb = sb("ones_sb", [1, 128])
        half_sb = sb("half_sb", [128, T])

        x_sb, x1_sb = sb("x_sb", [128, T, C]), sb("x1_sb", [128, T, C])
        modb, gb_sb = sb("modb", [C, 6]), sb("gb_sb", [C, 1])
        stats, mv, ve = sb("stats", [128, T, 6]), sb("mv", [128, T, 2]), sb("ve", [128, T])
        rstd = sb("rstd", [128, T])
        p_sb, p_rounded = in_one_place("p_sb", [128, 2, P_AT[T]], f32, "p_rounded", [128, 2, P_AT[T]], f32r)
        spare = p_sb[:, :, :].rearrange("p a n -> p (a n)")
        xn, att, x1_next = (tiles(spare[:, i * N:(i + 1) * N]) for i in range(3))
        conv, ke, qe, qT, kn = (spare[:, i * N:(i + 1) * N] for i in range(3, 8))
        lg, eq, mask = (spare[:, 3 * N + i * N // 2:3 * N + (i + 1) * N // 2].rearrange("p (t e) -> p t e", e=E)
                        for i in range(3))
        selT_all, h2_hi = in_one_place("selT_all", [128, 2 * N], bf16, "h2_hi", [C, N], f32r)
        h2T, h2_lo, selT = spare[:, 0:N], p_rounded[:, 0, N:2 * N], selT_all[0:H, 0:N]
        v_again, v_lo = (p[:, 1, 0:E * H * K].rearrange("p (e n) -> p e n", e=E) for p in (p_sb, p_rounded))
        v_sb = sb("v_sb", [128, T, H, K + 1])
        v_flat = v_sb[:, :, :, :].rearrange("p t h k -> p (t h k)")
        hn = v_flat[:, 0:T * (C + 1)].rearrange("p (t c) -> p t c", c=C + 1)
        yT, out_sb = v_flat[:, 2 * N:3 * N], tiles(v_flat[:, 3 * N:4 * N])
        o_sb = sb("o_sb", [128, T, H, K])
        qk = sb("qk", [128, 2, HP, N])
        hT, q_hl = in_one_place("hT", [C, N + 2], f32, "q_hl", [128, 3, N], f32r)
        k_hh = sb("k_hh", [128, 3, N], f32r)
        q_hm, k_l1 = sb("q_hm", [128, 2, N], f32r), sb("k_l1", [128, 2, N], f32r)
        spread_all = qk[:, :, :, :].rearrange("p a h n -> p (a h) n")
        z, oT = spread_all[:, 0:4], spread_all[:, 4:8]
        wmod_sb, sign_sb = spread_all[:, 7, 0:6 * C], spread_all[:, 6, 0:B * C]
        v_once = spread_all[:, 2:6].rearrange("p h n -> p (h n)").rearrange("p (e n) -> p e n", e=E)
        w_once = spread_all[:, 1, N - H * K:N], spread_all[:, 6, B * C:B * C + H * K]
        cst_once = spread_all[:, 0:2, :].rearrange("p h n -> p (h n)")[:, 0:sum(CONSTS.values()) - kept]

        def wmod_view(m):
            return wmod_sb[:, m * C:(m + 1) * C]
        kv_sb, rkv_sb = sb("kv_sb", [C, C]), sb("rkv_sb", [C, C])
        kvz = sb("kvz", [C, C + LH])
        ksum = sb("ksum", [C, 1])
        den = sb("den", [128, T * LH])
        top, best, sel = sb("top", [128, T * H]), sb("best", [128, T * H]), sb("sel", [128, T * H])
        gate = sb("gate", [128, T * H])
        m8, mrow = sb("m8", [128, 2, T]), sb("mrow", [T, 2, 128], f32r)
        rden = sb("rden", [128, 2, 4])
        PS = ctx.enter_context(nc.psum_tensor("PS", [128, 8 * 512], f32))

        def bank(i, n=1):
            return PS[:, i * 512:(i + n) * 512]

        def max_slot(h, t):
            return bank(4, 2) if h < 2 else bank(1, 2) if t >= 4 else bank(0)

        def score_slot(j):
            return (bank(3, 2), 0) if j < 4 else (bank(5), 512)

        def row_slot(h):
            return bank((4, 7)[h] if h < 2 else 0)[0:T, 0:128]

        def proj_slot(t):
            return bank(6 if t else 4, 2)

        block = ctx.enter_context(nc.Block())

        class Counts:

            def __init__(self, eng, first=0):
                self.eng, self.held, self.start = eng, None, {}
                self.ahead = 0
                self.target = eng.alloc_register(f"{eng.engine.name}_target")
                for per in sorted({p for p in per_batch.values() if p}):
                    self.start[per] = eng.alloc_register(f"{eng.engine.name}_start_{per}")
                    eng.reg_mov(self.start[per], first * per)

            def __call__(self, sem, count):
                per = per_batch[id(sem)]
                count += any(sem is s for s in one_ahead.values()) + self.ahead * per
                assert count > 0
                if self.held != (per, count):
                    self.eng.reg_add(self.target, self.start[per], count)
                    self.held = (per, count)
                return self.target

            def enter_loop(self):
                self.held = None

            def next_batch(self):
                self.held = None
                for per, register in self.start.items():
                    self.eng.reg_add(register, register, per)

        @block.sync
        def _(sp):
            x_v = x.rearrange("b (t p) c -> b p t c", p=128)
            out_v = out.rearrange("b (t p) c -> b p t c", p=128)
            sp.dma_start(x_sb[:], x_v[0, :, :, :]).then_inc(x_loaded, 16)
            small = ((cT_sb[:], c_t), (wmod_sb, w_mod), (cst[:], consts[:, 0:kept]), (cst_once, consts[:, kept:]),
                     (wqk_sb[:], w_qk_t), (bq_sb[:], b_q), (bk_sb[:], b_k), (lw_sb[:], lepe_w), (lb_sb[:], lepe_b),
                     (wg_sb[:], w_gate))
            assert len(small) == SMALL_LOADS
            for dst, src in small:
                sp.dma_start(dst, src).then_inc(small_loaded, 16)
            for dst, src in ((w_once[0], w_q), (w_once[1], w_k), (v_once, v_exp), (o_w[:], o_exp)):
                sp.dma_start(dst, src).then_inc(proj_loaded, 16)

            upto = Counts(sp)
            sp.wait_ge(att_ps, upto(att_ps, 1))
            sp.dma_start(v_again, v_exp).then_inc(v_loaded_again, 16)
            sp.wait_ge(x1_ready, upto(x1_ready, 1))
            sp.dma_start(x_sb[:], x_v[1, :, :, :]).then_inc(x_loaded, 16)

            def batch(b, load_next, again):
                for h in range(H):
                    sp.wait_ge(maxrow_ready, upto(maxrow_ready, h + 1))
                    sp.dma_start(q_hm[other(h).start:other(h).start + 1, h % 2, :].bitcast(f32),
                                 mrow[:, h % 2, :].bitcast(f32)).then_inc(maxrow_in, 16)
                if again:
                    sp.wait_ge(att_ps, upto(att_ps, 2))
                    sp.dma_start(v_again, v_exp).then_inc(v_loaded_again, 16)
                if load_next:
                    sp.wait_ge(x1_ready, upto(x1_ready, 2))
                    sp.dma_start(x_sb[:], x_v[b + 2, :, :, :]).then_inc(x_loaded, 16)
                sp.wait_ge(out_ready, upto(out_ready, 1))
                sp.dma_start(out_v[b, :, :, :], out_sb[:]).then_inc(out_stored, 16)
                upto.next_batch()

            upto.enter_loop()
            with sp.Fori(0, B - 2) as b:
                batch(b, True, True)
            batch(B - 2, False, True)
            batch(B - 1, False, False)
            sp.wait_ge(out_stored, 16 * B + 1)

        @block.gpsimd
        def _(pool):
            upto = Counts(pool)

            def deviation(k):
                pool.wait_ge(var_ready, upto(var_ready, k + 1))
                nc.gpsimd.tensor_tensor(rstd[:], ve[:], half_sb[:], ALU.pow).then_inc(rstd_ready, 1)

            def lower_values(experts):
                pool.wait_ge(v_loaded_again, upto(v_loaded_again, 16))
                for e in experts:
                    nc.gpsimd.tensor_tensor(v_lo[:, e, :], v_again[:, e, :], v_hi[:, e, :].bitcast(f32),
                                            ALU.subtract).then_inc(v_lo_ready, 1)

            def lower_keys(h):
                if h >= 2:
                    pool.wait_ge(k_lo_ready, upto(k_lo_ready, h))
                    pool.wait_ge(score_ps, upto(score_ps, T * (h - 1)))
                else:
                    pool.wait_ge(val_ready, upto(val_ready, T if h else 6))
                pool.wait_ge(k_hi_ready, upto(k_hi_ready, h + 1))
                nc.gpsimd.tensor_tensor(k_l1[own(h), h % 2, :], qk[own(h), 1, h // 2, :],
                                        k_hh[own(h), h % 3, :].bitcast(f32), ALU.subtract).then_inc(k_lo_ready, 1)

            def keep_x1():
                pool.wait_ge(x1_ready, upto(x1_ready, 1))
                pool.sem_inc(wait_carried, 1)
                nc.gpsimd.tensor_copy(x1_sb[:], x1_next).then_inc(x1_kept, 1)

            def batch(last):
                pool.wait_ge(gate_ready, upto(gate_ready, 1))
                for t in range(T):
                    if t == 6:
                        lower_keys(0)
                        pool.wait_ge(k_lo_ready, upto(k_lo_ready, 1))
                    done = PICKS[VALUE_ORDER.index((t, E - 1)) + 1]
                    pool.wait_ge(val_picked, upto(val_picked, done))
                    v_t = v_sb[:, t, :, 0:K]
                    g_t = gate[:, t * H:(t + 1) * H].unsqueeze(2).broadcast_to([128, H, K])
                    nc.gpsimd.tensor_tensor(v_t, v_t, g_t, ALU.mult).then_inc(val_ready, 1)
                for h in range(1, H):
                    lower_keys(h)
                if not last:
                    pool.wait_ge(k_lo_ready, upto(k_lo_ready, H))
                    upto.ahead = 1
                    deviation(0)
                    lower_values(range(E // 2))
                    deviation(1)
                    lower_values(range(E // 2, E))
                    upto.ahead = 0
                    pool.wait_ge(out_ready, upto(out_ready, 1))
                    upto.ahead = 1
                    keep_x1()
                    upto.ahead = 0
                upto.next_batch()

            deviation(0)
            deviation(1)
            keep_x1()
            pool.wait_ge(w_hi_ready, 1)
            for i in range(2):
                nc.gpsimd.tensor_tensor(w_lo[:, i, :], w_once[i], w_hi[:, i, :].bitcast(f32),
                                        ALU.subtract).then_inc(w_lo_ready, 1)
            pool.wait_ge(v_hi_ready, 1)
            lower_values(range(E))
            upto.enter_loop()
            with pool.Fori(0, B - 1):
                batch(False)
            batch(True)

        @block.scalar
        def _(act):
            act.wait_ge(small_loaded, 16 * SMALL_LOADS)
            nc.scalar.activation(sig_sb[:], cT_sb[:], ACT.Exp, scale=-1.0).then_inc(silu_exp_ready, 1)
            upto = Counts(act)

            def modulated():
                act.wait_ge(xnT_ps, upto(xnT_ps, 1))
                act.wait_ge(mod_picked, upto(mod_picked, 1))
                nc.scalar.activation(hT[:, 1:N + 1], bank(0, 2), ACT.Identity,
                                                      scale=modb[:, MOD_CA:MOD_CA + 1],
                                                      bias=modb[:, MOD_SA:MOD_SA + 1]).then_inc(hT_ready, 1)
                act.wait_ge(hT_ready, upto(hT_ready, 1))
                nc.scalar.activation(conv[:], hT[:, 1:N + 1], ACT.Identity,
                                                      scale=lw_sb[:, 1:2], bias=lb_sb[:]).then_inc(conv_mid, 1)

            def h_natural():
                act.wait_ge(hn_ps, upto(hn_ps, 1))
                nc.scalar.activation(hn[:, :, 0:C], tiles(bank(6, 2)), ACT.Copy).then_inc(hn_ready, 1)

            def exp_keys():
                act.wait_ge(k_ps, upto(k_ps, 1))
                nc.scalar.activation(ke, bank(6, 2), ACT.Relu, scale=-1.0).then_inc(kneg_ready, 1)
                act.wait_ge(kneg_ready, upto(kneg_ready, 1))
                nc.scalar.activation(ke, ke, ACT.Exp, scale=-1.0).then_inc(kexp_ready, 1)

            def exp_queries():
                act.wait_ge(q_ps, upto(q_ps, 1))
                nc.scalar.activation(qe, bank(6, 2), ACT.Relu, scale=-1.0, bias=bqm_sb[:]).then_inc(qneg_ready, 1)
                act.wait_ge(qneg_ready, upto(qneg_ready, 1))
                nc.scalar.activation(qe, qe, ACT.Exp, scale=-1.0).then_inc(qexp_ready, 1)

            def modulated_2():
                act.wait_ge(xnT_ps, upto(xnT_ps, 2))
                nc.scalar.activation(h2T, bank(6, 2), ACT.Identity,
                                                       scale=modb[:, MOD_CB:MOD_CB + 1],
                                                       bias=modb[:, MOD_SB:MOD_SB + 1]).then_inc(h2T_ready, 1)
                act.wait_ge(h2T_ready, upto(h2T_ready, 1))
                nc.scalar.activation(h2_hi[:], h2T, ACT.Copy).then_inc(h2_hi_ready, 1)

            def double(h):
                act.wait_ge(oT_ps, upto(oT_ps, h // 2 + 1))
                if h >= 4:
                    act.wait_ge(z_ready, upto(z_ready, EC * (h - 3)))
                src = bank(2, 2)[K * (h % 2):K * (h % 2 + 1)]
                nc.scalar.activation(oT[0:K, h % 4, :], src, ACT.Copy)
                nc.scalar.activation(oT[K:2 * K, h % 4, :], src, ACT.Copy).then_inc(oT_ready, 1)

            def batch(last):
                def upper_parts(h, step):
                    q, k = qk[own(h), 0, h // 2, :], qk[own(h), 1, h // 2, :]
                    if step == 0:
                        if h >= 3:
                            act.wait_ge(score_ps, upto(score_ps, T * (h - 2)))
                        nc.scalar.activation(q_hl[own(h), h % 3, :], q, ACT.Copy).then_inc(q_hi_ready, 1)
                    elif step == 1:
                        nc.scalar.activation(k_hh[own(h), h % 3, :], k, ACT.Copy).then_inc(k_hi_ready, 1)
                    else:
                        nc.scalar.activation(k_hh[other(h), h % 3, :], k, ACT.Copy).then_inc(k_hh_ready, 1)

                def projected(t):
                    act.wait_ge(proj_ps, upto(proj_ps, t + 1))
                    nc.scalar.activation(qk[:, t % 2, t // 2, :], proj_slot(t), ACT.Copy).then_inc(proj_ready, 1)

                projected(0)
                projected(1)
                act.wait_ge(proj_ready, upto(proj_ready, 2))
                upper_parts(0, 0)
                act.wait_ge(top_ready, upto(top_ready, 1))
                nc.scalar.activation(gate[:], top[:], ACT.Exp, scale=-1.0).then_inc(topexp_ready, 1)
                upper_parts(0, 1)
                upper_parts(0, 2)
                act.wait_ge(out_stored, upto(out_stored, 0))
                for n, (t, e) in enumerate(VALUE_ORDER):
                    if e == 0:
                        act.wait_ge(val_ps, upto(val_ps, n + 1))
                        nc.scalar.activation(v_sb[:, t, :, 0:K], tiles(bank(n % 4), K), ACT.Copy).then_inc(val_first, 1)
                    if n in PROJECTED:
                        projected(PROJECTED[n])
                    if n in (10, 12, 14):
                        upper_parts(1, n // 2 - 5)
                    if n in (40, 42, 44):
                        act.wait_ge(proj_ready, upto(proj_ready, 4))
                        upper_parts(2, n // 2 - 20)
                act.wait_ge(proj_ready, upto(proj_ready, 2 * HP))
                act.wait_ge(x1_kept, upto(x1_kept, 1))
                for h in range(H):
                    if h >= 2:
                        act.wait_ge(av_ps, upto(av_ps, 2 * (h - 1)))
                    for n, j in enumerate(KEY_ORDER):
                        act.wait_ge(score_ps, upto(score_ps, T * h + n + 1))
                        slot, off = score_slot(j)
                        src = slot[:, 128 * j - off:N - off]
                        nc.scalar.activation(p_sb[:, h % 2, P_AT[j]:P_AT[j + 1]], src, ACT.Exp,
                                             scale=SCALE).then_inc(prob_ready, 1)
                        if n in (1, 3, 5) and 3 <= h + 2 < H:
                            upper_parts(h + 2, n // 2)
                        if h == H - 1 and n == 1:
                            act.wait_ge(selT_ps, upto(selT_ps, 1))
                            nc.scalar.activation(selT[:], bank(0, 2)[0:H], ACT.Copy).then_inc(selT_ready, 1)
                for what in (double, 0), (double, 1), modulated, h_natural, exp_keys, (double, 2), (double, 3), \
                        exp_queries, (double, 4), (double, 5), (double, 6), (double, 7), modulated_2:
                    if isinstance(what, tuple):
                        what[0](what[1])
                    elif not last:
                        upto.ahead = 1
                        what()
                        upto.ahead = 0
                act.wait_ge(z_used, upto(z_used, H * EC))
                act.wait_ge(gb_ready, upto(gb_ready, 1))
                nc.scalar.activation(yT, bank(0, 2), ACT.Copy, scale=gb_sb[:]).then_inc(yT_ready, 1)
                upto.next_batch()

            modulated()
            h_natural()
            exp_keys()
            exp_queries()
            act.wait_ge(proj_loaded, 16 * 4)
            nc.scalar.activation(w_hi[:, 0, :], w_once[0], ACT.Copy)
            nc.scalar.activation(w_hi[:, 1, :], w_once[1], ACT.Copy).then_inc(w_hi_ready, 1)
            nc.scalar.activation(v_hi[:], v_once, ACT.Copy).then_inc(v_hi_ready, 1)
            modulated_2()
            upto.enter_loop()
            with act.Fori(0, B - 1):
                batch(False)
            batch(True)

        @block.vector
        def _(dve):
            v = nc.vector

            upto = Counts(dve)
            base, links = 0, [0]
            for ahead in one_ahead.values():
                dve.sem_inc(ahead, 1)

            def link(ins):
                links[0] += 1
                ins.then_inc(dve_step, 1)
                dve.wait_ge(dve_step, upto(dve_step, base + links[0] - upto.ahead * DVE_STEPS))

            def variances(src):
                for t in range(T):
                    last = v.bn_stats(stats[:, t, :], src[:, t, :])
                link(last)
                dve.sem_inc(wait_carried, 1)
                for t in range(T):
                    last = v.bn_aggr(mv[:, t, :], stats[:, t, :])
                link(last)
                v.tensor_scalar(ve[:], mv[:, :, 1], EPS, None, ALU.add).then_inc(var_ready, 1)

            def normalised(src, k):
                dve.wait_ge(rstd_ready, upto(rstd_ready, k + 1))
                for t in range(T):
                    v.tensor_scalar(xn[:, t, :], src[:, t, :], mv[:, t, 0:1], rstd[:, t:t + 1],
                                                     ALU.subtract, ALU.mult).then_inc(xn_ready, 1)

            def first_norm(nb):
                link(v.tensor_copy(modb[:], mod_sb[:, :, bass.ds(nb, 1)].rearrange("p m b -> p (m b)")))
                dve.sem_inc(mod_picked, 1)
                dve.wait_ge(x_loaded, upto(x_loaded, 16))
                variances(x_sb)

            def first_norm_2():
                normalised(x_sb, 0)

            def h_edges():
                v.memset(hT[:, 0:1], 0.0)
                link(v.memset(hT[:, N + 1:N + 2], 0.0))
                v.memset(hn[:, :, C:C + 1], 1.0)

            def keys():
                dve.wait_ge(kexp_ready, upto(kexp_ready, 1))
                v.scalar_tensor_tensor(kn, bank(6, 2), 1.0, ke, ALU.add, ALU.max).then_inc(k_ready, 1)

            def queries():
                dve.wait_ge(qexp_ready, upto(qexp_ready, 1))
                v.scalar_tensor_tensor(qT, bank(6, 2), bq1_sb[:], qe, ALU.add, ALU.max).then_inc(qT_ready, 1)

            def keys_values():
                dve.wait_ge(kv_ps, upto(kv_ps, 1))
                v.tensor_tensor(kv_sb[:], bank(6)[:, 0:C], const("same_head"), ALU.mult).then_inc(kv_ready, 1)
                link(v.tensor_copy(ksum[:], bank(6)[:, C:C + 1]))
                v.tensor_scalar(kvz[:, C:C + LH], const("head_of"), ksum[:], None, ALU.mult).then_inc(kmean_ready, 1)

            def rotated():
                dve.wait_ge(rkv_ps, upto(rkv_ps, 1))
                v.tensor_copy(rkv_sb[:], bank(7)[:, 0:C]).then_inc(rkv_ready, 1)

            def rotated_back():
                dve.wait_ge(rrkv_ps, upto(rrkv_ps, 1))
                v.tensor_copy(kvz[:, 0:C], bank(6)[:, 0:C]).then_inc(rrkv_ready, 1)
                dve.wait_ge(den_ps, upto(den_ps, 1))
                v.tensor_scalar(den[:], bank(7)[:, 0:T * LH], 1e-6, None, ALU.add).then_inc(den_ready, 1)
                dve.wait_ge(den_ready, upto(den_ready, 1))
                link(v.reciprocal(den[:], den[:]))

            def convolved():
                dve.wait_ge(conv_mid, upto(conv_mid, 1))
                link(v.scalar_tensor_tensor(conv[:], hT[:, 0:N], lw_sb[:, 0:1], conv[:], ALU.mult, ALU.add))
                v.scalar_tensor_tensor(conv[:], hT[:, 2:N + 2], lw_sb[:, 2:3], conv[:],
                                                          ALU.mult, ALU.add).then_inc(conv_ready, 1)

            def attended():
                dve.wait_ge(att_ps, upto(att_ps, 1))
                att_h = att[:].rearrange("p t (h d) -> p (t h) d", d=LD)
                v.tensor_tensor(att_h, tiles(bank(6, 2), LD), den[:].unsqueeze(2).broadcast_to([128, T * LH, LD]),
                                ALU.mult).then_inc(att_ready, 1)

            def residual():
                dve.wait_ge(conv_ps, upto(conv_ps, 1))
                link(v.tensor_tensor(att[:], att[:], tiles(bank(6, 2)), ALU.add))

            def residual_2(nb):
                link(v.tensor_tensor(att[:], att[:], ga_row[:, bass.ds(nb, 1), :].broadcast_to([128, T, C]), ALU.mult))

            def residual_3():
                v.tensor_tensor(x1_next[:], att[:], x_sb[:], ALU.add).then_inc(x1_ready, 1)

            def residual_stats():
                dve.wait_ge(x1_ready, upto(x1_ready, 1))
                variances(x1_next)

            def second_norm():
                normalised(x1_next, 1)

            def lower_h2():
                dve.wait_ge(h2_hi_ready, upto(h2_hi_ready, 1))
                v.tensor_tensor(h2_lo, h2T, h2_hi[:].bitcast(f32), ALU.subtract).then_inc(h2_lo_ready, 1)

            def batch(b, last):
                dve.wait_ge(logit_ps, upto(logit_ps, 1))
                link(v.tensor_scalar(lg[:], tiles(bank(2), E), SATURATED, None, ALU.min))
                v.tensor_reduce(top[:], lg[:], AX.X, ALU.max).then_inc(top_ready, 1)
                dve.wait_ge(top_ready, upto(top_ready, 1))
                link(v.tensor_tensor(eq[:], lg[:], top[:].unsqueeze(2).broadcast_to([128, T * H, E]), ALU.is_equal))
                link(v.tensor_tensor(eq[:], eq[:], const("rank").unsqueeze(1).broadcast_to([128, T * H, E]), ALU.mult))
                link(v.tensor_reduce(best[:], eq[:], AX.X, ALU.max))
                v.tensor_scalar(sel[:], best[:], -1.0, float(E), ALU.mult, ALU.add)
                link(v.tensor_tensor(mask[:], eq[:], best[:].unsqueeze(2).broadcast_to([128, T * H, E]), ALU.is_equal))
                dve.wait_ge(topexp_ready, upto(topexp_ready, 1))
                link(v.tensor_scalar(gate[:], gate[:], 1.0, None, ALU.add))
                v.reciprocal(gate[:], gate[:]).then_inc(gate_ready, 1)

                def maxima(h, ns):
                    for n in ns:
                        t = MAX_ORDER[n]
                        dve.wait_ge(max_ps, upto(max_ps, T * h + n + 1))
                        v.tensor_reduce(m8[:, h % 2, t:t + 1], max_slot(h, t)[:, 0:128 * (t + 1)], AX.X,
                                        ALU.max).then_inc(max_ready, 1)

                def max_row(h):
                    dve.wait_ge(maxrow_ps, upto(maxrow_ps, h + 1))
                    if h >= 2:
                        dve.wait_ge(maxrow_in, upto(maxrow_in, 16 * (h - 1)))
                    v.tensor_scalar(mrow[:, h % 2, :], row_slot(h), -1.0, None,
                                                         ALU.mult).then_inc(maxrow_ready, 1)

                def lower_queries(h):
                    dve.wait_ge(q_hi_ready, upto(q_hi_ready, h + 1))
                    v.tensor_tensor(q_hl[other(h), h % 3, :], qk[own(h), 0, h // 2, :],
                                    q_hl[own(h), h % 3, :].bitcast(f32), ALU.subtract).then_inc(q_lo_ready, 1)

                def upper_queries(h):
                    if h >= 2:
                        dve.wait_ge(score_ps, upto(score_ps, T * (h - 1)))
                    v.tensor_copy(q_hm[own(h), h % 2, :], q_hl[own(h), h % 3, :].bitcast(f32)).then_inc(q_hm_ready, 1)

                for n, (t, e) in enumerate(VALUE_ORDER):
                    if e == 1:
                        dve.wait_ge(val_first, upto(val_first, t + 1))
                    elif e:
                        dve.wait_ge(val_picked, upto(val_picked, PICKS[n - 1]))
                    if e:
                        dve.wait_ge(val_ps, upto(val_ps, n + 1))
                        dve.sem_inc(wait_carried, 1)
                        pick = mask[:, t * H:(t + 1) * H, e:e + 1].bitcast(u32).broadcast_to([128, H, K])
                        v.copy_predicated(v_sb[:, t, :, 0:K], pick, tiles(bank(n % 4), K)).then_inc(val_picked, 1)
                    if n in VALUES_MAX:
                        maxima(VALUES_MAX[n][0], (VALUES_MAX[n][1],))
                    if n in VALUES_ROW:
                        max_row(VALUES_ROW[n])
                    if n == 6:
                        lower_queries(0)
                        upper_queries(0)
                    if n == 30:
                        lower_queries(1)
                    if n == 53:
                        upper_queries(1)
                v.memset(v_sb[:, :, :, K:K + 1], 1.0).then_inc(mask_ready, 1)

                def heads_out(h, half):
                    dve.wait_ge(av_ps, upto(av_ps, 2 * h + half + 1))
                    src = bank(6 + half)[:, 0:4 * (K + 1)].rearrange("p (t k) -> p t k", k=K + 1)
                    link(v.reciprocal(rden[:, half, :], src[:, :, K]))
                    g = gate[:].rearrange("p (t h) -> p t h", h=H)[:, 4 * half:4 * half + 4, h]
                    link(v.tensor_tensor(rden[:, half, :], rden[:, half, :], g, ALU.mult))
                    v.tensor_tensor(o_sb[:, 4 * half:4 * half + 4, h, :], src[:, :, 0:K],
                                    rden[:, half, :].unsqueeze(2).broadcast_to([128, 4, K]),
                                    ALU.mult).then_inc(o_ready, 1)

                lower_queries(2)
                maxima(2, range(T))
                for h in range(1, H):
                    if 3 <= h + 1 < H:
                        maxima(h + 1, range(4))
                    if h + 1 < H:
                        upper_queries(h + 1)
                    if 3 <= h + 1 < H:
                        maxima(h + 1, (4, 5))
                    if h == H - 1:
                        v.tensor_copy(gb_sb[:], modb[:, MOD_GB:MOD_GB + 1]).then_inc(gb_ready, 1)
                        dve.wait_ge(gb_ready, upto(gb_ready, 1))
                        if not last:
                            upto.ahead = 1
                            first_norm(b + 1)
                            upto.ahead = 0
                    heads_out(h - 1, 0)
                    if 3 <= h + 1 < H:
                        maxima(h + 1, (6, 7))
                    if h + 1 < H:
                        max_row(h + 1)
                    if h + 2 < H:
                        lower_queries(h + 2)
                    heads_out(h - 1, 1)
                if not last:
                    upto.ahead = 1
                    first_norm_2()
                    upto.ahead = 0
                heads_out(H - 1, 0)

                between = {3: [h_edges], 6: [keys], 10: [queries], 11: [convolved], 13: [keys_values], 15: [rotated],
                           17: [rotated_back], 19: [attended], 21: [residual], 22: [lambda: residual_2(b + 1)],
                           23: [residual_3], 25: [residual_stats], 27: [second_norm]}
                for n in range(H * EC):
                    h, c = divmod(n, EC)
                    if c == 0:
                        dve.wait_ge(oT_ready, upto(oT_ready, h + 1))
                        dve.wait_ge(selB_ps, upto(selB_ps, h + 1))
                    if n >= 4:
                        dve.wait_ge(z_used, upto(z_used, n - 3))
                    v.scalar_tensor_tensor(z[:, n % 4, :], bank(4, 2), const("expert_of")[:, c:c + 1], oT[:, h % 4, :],
                                           ALU.is_equal, ALU.mult).then_inc(z_ready, 1)
                    if n == 2:
                        heads_out(H - 1, 1)
                    if not last:
                        upto.ahead = 1
                        for step in between.get(n, ()):
                            step()
                        upto.ahead = 0
                if not last:
                    upto.ahead = 1
                    lower_h2()
                    upto.ahead = 0
                dve.wait_ge(y_ps, upto(y_ps, 1))
                dve.wait_ge(x1_kept, upto(x1_kept, 1))
                v.tensor_tensor(out_sb, x1_sb[:], tiles(bank(2, 2)), ALU.add).then_inc(out_ready, 1)
                if not last:
                    assert links[0] == DVE_STEPS, links[0]
                upto.next_batch()

            v.memset(ones_sb[:], 1.0)
            v.memset(half_sb[:], -0.5)
            dve.wait_ge(x_loaded, upto(x_loaded, 16))
            variances(x_sb)
            dve.wait_ge(small_loaded, 16 * SMALL_LOADS)
            v.tensor_scalar(bq1_sb[:], bq_sb[:], 1.0, None, ALU.add)
            v.tensor_scalar(bqm_sb[:], bq_sb[:], -1.0, None, ALU.mult)
            dve.wait_ge(silu_exp_ready, 1)
            link(v.tensor_scalar(sig_sb[:], sig_sb[:], 1.0, None, ALU.add))
            link(v.reciprocal(sig_sb[:], sig_sb[:]))
            v.tensor_tensor(silu_sb[:], sig_sb[:], cT_sb[:], ALU.mult).then_inc(silu_ready, 1)
            first_norm_2()

            def clamp(ap, sign):
                link(v.tensor_scalar(sign, ap, 0.0, 2.0, ALU.is_ge, ALU.mult))
                link(v.tensor_scalar(sign, sign, -1.0, None, ALU.add))
                link(v.tensor_tensor(ap, ap, sign, ALU.mult))
                link(v.tensor_scalar(ap, ap, 0.25, None, ALU.max))
                link(v.tensor_tensor(ap, ap, sign, ALU.mult))

            dve.wait_ge(mod_ps_ready, 1)
            link(v.tensor_copy(mod_sb[:].rearrange("p m b -> p (m b)"), bank(2)[:, 0:6 * B]))
            for m in (MOD_CA, MOD_CB):
                link(v.tensor_scalar(mod_sb[:, m, :], mod_sb[:, m, :], 1.0, None, ALU.add))
            clamp(mod_sb[:, MOD_GB, :], sign_sb[:, 0:B])
            link(v.tensor_copy(modb[:], mod_sb[:, :, 0]))
            dve.sem_inc(mod_picked, 1)
            v.tensor_copy(ident_b[:], ident)
            v.tensor_copy(causal_b[:], const("causal"))
            v.tensor_copy(causal_tb[:], const("causal_t"))
            v.tensor_copy(row_of_b[:], const("row_of", H))
            link(v.tensor_copy(ga_row[:].rearrange("p b c -> p (b c)"), bank(3)))
            clamp(ga_row[:].rearrange("p b c -> p (b c)"), sign_sb[:])
            v.memset(q_hm[:].bitcast(f32), 0.0)
            link(v.memset(k_l1[:].bitcast(f32), 0.0))
            for h in range(2):
                v.memset(k_l1[other(h).start:other(h).start + 1, h, :].bitcast(f32), 1.0)
            h_edges()
            keys()
            queries()
            keys_values()
            rotated()
            convolved()
            rotated_back()
            attended()
            residual()
            residual_2(0)
            residual_3()
            residual_stats()
            second_norm()
            lower_h2()
            base, links[0] = links[0], 0
            upto.enter_loop()
            with dve.Fori(0, B - 1) as b:
                batch(b, False)
            links[0] = 0
            batch(B - 1, True)

        @block.tensor
        def _(pe):
            mm = nc.tensor.matmul
            pe.wait_ge(silu_ready, 1)
            for m in range(6):
                mm(bank(2)[:, m * B:(m + 1) * B], wmod_view(m), silu_sb[:], start=True, stop=True)
            for i in range(B):
                last = mm(bank(3)[:, i * C:(i + 1) * C], silu_sb[:, i:i + 1].broadcast_to([C, 128]), wmod_view(MOD_GA),
                          start=True, stop=True)
            last.then_inc(mod_ps_ready, 1)

            upto = Counts(pe)

            def transpose_tiles(first, src, signal, width=128, waits=None):
                for t in range(T):
                    if waits:
                        waits(t)
                    last = nc.tensor.transpose(bank(first, 2)[0:width, t * 128:(t + 1) * 128], src(t), ident)
                last.then_inc(signal, 1)


            def x_turned():
                transpose_tiles(0, lambda t: xn[:, t, :], xnT_ps,
                                waits=lambda t: pe.wait_ge(xn_ready, upto(xn_ready, t + 1)))

            def h_turned():
                pe.wait_ge(hT_ready, upto(hT_ready, 1))
                transpose_tiles(6, lambda t: hT[:, 1 + t * 128:1 + (t + 1) * 128], hn_ps)

            def keys():
                pe.wait_ge(hn_ready, upto(hn_ready, 1))
                for i in range(2):
                    mm(bank(6 + i), ones_sb[:], bk_sb[:].unsqueeze(1).broadcast_to([1, 4, C]), start=True, stop=True)
                    for t in range(4):
                        n = 4 * i + t
                        last = mm(bank(6 + i)[:, t * C:(t + 1) * C], hT[:, 1 + n * 128:1 + (n + 1) * 128],
                                  wqk_sb[:, C:2 * C], start=False, stop=True, skip_group_check=True)
                last.then_inc(k_ps, 1)

            def queries():
                pe.wait_ge(k_ready, upto(k_ready, 1))
                for i in range(2):
                    last = mm(bank(6 + i), wqk_sb[:, 0:C], hT[:, 1 + i * 512:1 + (i + 1) * 512], start=True, stop=True)
                last.then_inc(q_ps, 1)

            def keys_values():
                pe.wait_ge(qT_ready, upto(qT_ready, 1))
                for t in range(T):
                    last = mm(bank(6)[:, 0:C + 1], kn[:, t * C:(t + 1) * C], hn[:, t, :], start=t == 0, stop=t == T - 1)
                last.then_inc(kv_ps, 1)

            def rotated():
                pe.wait_ge(kv_ready, upto(kv_ready, 1))
                mm(bank(7)[:, 0:C], const("rot_t"), kv_sb[:], start=True, stop=True).then_inc(rkv_ps, 1)

            def rotated_back():
                pe.wait_ge(rkv_ready, upto(rkv_ready, 1))
                pe.wait_ge(kmean_ready, upto(kmean_ready, 1))
                mm(bank(6)[:, 0:C], const("rot"), rkv_sb[:], start=True, stop=True).then_inc(rrkv_ps, 1)
                for t in range(T):
                    last = mm(bank(7)[:, t * LH:(t + 1) * LH], qT[:, t * 128:(t + 1) * 128], kvz[:, C:C + LH],
                              start=True, stop=True)
                last.then_inc(den_ps, 1)

            def attended():
                pe.wait_ge(rrkv_ready, upto(rrkv_ready, 1))
                pe.wait_ge(den_ready, upto(den_ready, 1))
                for t in range(T):
                    last = mm(bank(6, 2)[:, t * C:(t + 1) * C], qT[:, t * 128:(t + 1) * 128], kvz[:, 0:C],
                              start=True, stop=True)
                last.then_inc(att_ps, 1)

            def conv_turned():
                pe.wait_ge(conv_ready, upto(conv_ready, 1))
                pe.wait_ge(att_ready, upto(att_ready, 1))
                transpose_tiles(6, lambda t: conv[:, t * 128:(t + 1) * 128], conv_ps)

            def x1_turned():
                transpose_tiles(6, lambda t: xn[:, t, :], xnT_ps,
                                waits=lambda t: pe.wait_ge(xn_ready, upto(xn_ready, T + t + 1)))

            def projection(t):
                if t >= 2:
                    pe.wait_ge(proj_ready, upto(proj_ready, t))
                for w, h2, start in ((w_hi, h2_hi, True), (w_lo, h2_hi, False), (w_hi, h2_lo, False)):
                    for i in range(2):
                        last = mm(proj_slot(t)[:, i * 512:(i + 1) * 512], w[:, t % 2, t // 2 * 128:(t // 2 + 1) * 128],
                                  h2[:, i * 512:(i + 1) * 512], start=start, stop=h2 is h2_lo)
                last.then_inc(proj_ps, 1)

            def batch(last_batch):
                def max_tile(h, n):
                    t = MAX_ORDER[n]
                    if (h, n) == (0, 0):
                        pe.wait_ge(proj_ready, upto(proj_ready, 1))
                    elif h < 2:
                        pe.wait_ge(max_ready, upto(max_ready, T * h + n))
                        if n == 0:
                            pe.wait_ge(maxrow_ready, upto(maxrow_ready, 1))
                    elif n >= 2:
                        pe.wait_ge(max_ready, upto(max_ready, T * h + n - 1))
                    elif n == 0:
                        pe.wait_ge(max_ready, upto(max_ready, T * h))
                        pe.wait_ge(maxrow_ready, upto(maxrow_ready, h))
                    dst = max_slot(h, t)
                    if n == 0:
                        pe.wait_ge(q_lo_ready, upto(q_lo_ready, h + 1))
                        pe.wait_ge(k_hh_ready, upto(k_hh_ready, h + 1))
                    q = q_hl[:, h % 3, t * 128:(t + 1) * 128]
                    w = 128 * (t + 1)
                    for at in range(0, w, 512):
                        to = min(at + 512, w)
                        mm(dst[:, at:to], q, k_hh[:, h % 3, at:to], start=True, stop=True)

                def max_tiles(h, ns):
                    for n in ns:
                        max_tile(h, n)
                    for n in ns:
                        dst, w = max_slot(h, MAX_ORDER[n]), 128 * (MAX_ORDER[n] + 1)
                        mm(dst[:, w - 128:w], ident_b[:], causal_b[:], start=False, stop=True,
                           skip_group_check=True).then_inc(max_ps, 1)

                def max_row(h):
                    pe.wait_ge(max_ready, upto(max_ready, T * (h + 1)))
                    if h == 1:
                        pe.wait_ge(maxrow_in, upto(maxrow_in, 16))
                        pe.wait_ge(proj_ready, upto(proj_ready, 2 * HP))
                    nc.tensor.transpose(row_slot(h), m8[:, h % 2, :], ident).then_inc(maxrow_ps, 1)

                def score_tile(h, n):
                    j = KEY_ORDER[n]
                    if n >= 2:
                        pe.wait_ge(prob_ready, upto(prob_ready, T * h + n - 1))
                    else:
                        if h:
                            pe.wait_ge(prob_ready, upto(prob_ready, T * h))
                        pe.wait_ge(maxrow_in, upto(maxrow_in, 16 * (h + 1)))
                    dst, off = score_slot(j)
                    if n == 0:
                        pe.wait_ge(q_hm_ready, upto(q_hm_ready, h + 1))
                        pe.wait_ge(k_lo_ready, upto(k_lo_ready, h + 1))
                    edge = max(512, 128 * (j + 1)) if j < 4 else N
                    spans = [(at, to) for at, to in ((128 * j, edge), (edge, N)) if at < to]
                    for k, q, start in ((k_hh[:, h % 3], q_hl[:, h % 3], True), (k_l1[:, h % 2], q_hm[:, h % 2], False)):
                        for at, to in spans:
                            mm(dst[:, at - off:to - off], k[:, j * 128:(j + 1) * 128], q[:, at:to], start=start,
                               stop=True, skip_group_check=not start)

                def score_tiles(h, ns):
                    for n in ns:
                        score_tile(h, n)
                    for n in ns:
                        j = KEY_ORDER[n]
                        dst, off = score_slot(j)
                        mm(dst[:, 128 * j - off:128 * (j + 1) - off], ident_b[:], causal_tb[:], start=False, stop=True,
                           skip_group_check=True).then_inc(score_ps, 1)

                def av_tile(h, i):
                    need = 1 + max(KEY_ORDER.index(j) for j in range(i + 1))
                    pe.wait_ge(prob_ready, upto(prob_ready, T * h + need))
                    half = i // 4
                    if i % 4 == 0 and h:
                        pe.wait_ge(o_ready, upto(o_ready, 2 * (h - 1) + half + 1))
                    for j in range(i + 1):
                        at = P_AT[j] + 128 * (i - j)
                        last = mm(bank(6 + half)[:, (i % 4) * (K + 1):(i % 4 + 1) * (K + 1)],
                                  p_sb[:, h % 2, at:at + 128], v_sb[:, j, h, :], start=j == 0, stop=j == i)
                    if i % 4 == 3:
                        last.then_inc(av_ps, 1)

                pe.wait_ge(out_ready, upto(out_ready, 0))
                for t in range(T):
                    last = mm(bank(2)[:, t * H * E:(t + 1) * H * E], h2T[:, t * 128:(t + 1) * 128], wg_sb[:],
                              start=True, stop=True)
                last.then_inc(logit_ps, 1)
                for n, (t, e) in enumerate(VALUE_ORDER):
                    if n == 2:
                        pe.wait_ge(top_ready, upto(top_ready, 1))
                    if n >= 4:
                        t4, e4 = VALUE_ORDER[n - 4]
                        if e4:
                            pe.wait_ge(val_picked, upto(val_picked, PICKS[n - 3]))
                        else:
                            pe.wait_ge(val_first, upto(val_first, t4 + 1))
                    if t == 0:
                        pe.wait_ge(v_lo_ready, upto(v_lo_ready, e + 1))
                        if e == 0:
                            pe.wait_ge(h2_lo_ready, upto(h2_lo_ready, 1))
                    hi, lo = (part[:, t * 128:(t + 1) * 128] for part in (h2_hi, h2_lo))
                    mm(bank(n % 4), hi, v_hi[:, e, :], start=True, stop=False)
                    mm(bank(n % 4), hi, v_lo[:, e, :], start=False, stop=False)
                    mm(bank(n % 4), lo, v_hi[:, e, :], start=False, stop=True).then_inc(val_ps, 1)
                    if n in PROJECTED:
                        projection(PROJECTED[n])
                    if n in VALUES_MAX:
                        max_tiles(VALUES_MAX[n][0], (VALUES_MAX[n][1],))
                    if n in VALUES_ROW:
                        max_row(VALUES_ROW[n])

                pe.wait_ge(val_picked, upto(val_picked, T * (E - 1)))
                pe.wait_ge(val_first, upto(val_first, T))
                pe.wait_ge(max_ready, upto(max_ready, 2 * T))
                for h in range(H):
                    if h == 1:
                        pe.wait_ge(val_ready, upto(val_ready, T))
                        pe.wait_ge(mask_ready, upto(mask_ready, 1))
                        pe.wait_ge(maxrow_ready, upto(maxrow_ready, 2))
                    if h == H - 1:
                        pe.wait_ge(max_ready, upto(max_ready, T * H))
                        pe.wait_ge(maxrow_ready, upto(maxrow_ready, H))
                        transpose_tiles(0, lambda t: sel[:, t * H:(t + 1) * H], selT_ps, width=H)
                    for what, ns in HEAD_ORDER if h else FIRST_ORDER:
                        if what == "max" and (h == 0 or 3 <= h + 1 < H):
                            max_tiles(h + 1 if h else 2, ns)
                        if what == "row" and h + 1 < H:
                            max_row(h + 1)
                        if what == "score":
                            score_tiles(h, ns)
                        if what == "values" and h >= 1:
                            for n in ns:
                                av_tile(h - 1, n)

                def turn_pair(h):
                    if h:
                        pe.wait_ge(oT_ready, upto(oT_ready, h))
                    pe.wait_ge(o_ready, upto(o_ready, 2 * (h + 2)))
                    transpose_tiles(2, lambda t: o_sb[:, t, h:h + 2, :].rearrange("p h k -> p (h k)"), oT_ps)

                def spread_experts(h):
                    if h:
                        pe.wait_ge(z_ready, upto(z_ready, EC * h))
                    for i in range(2):
                        last = mm(bank(4 + i), row_of_b[:, h * 128:(h + 1) * 128], selT[:, i * 512:(i + 1) * 512],
                                  start=True, stop=True)
                    last.then_inc(selB_ps, 1)

                pe.wait_ge(prob_ready, upto(prob_ready, T * H))
                turn_pair(0)
                pe.wait_ge(selT_ready, upto(selT_ready, 1))
                spread_experts(0)
                for n in range(4):
                    av_tile(H - 1, n)
                if not last_batch:
                    upto.ahead = 1
                    x_turned()
                    upto.ahead = 0
                for n in range(4, T):
                    av_tile(H - 1, n)
                between = {0: h_turned, 2: keys, 5: queries, 9: keys_values, 11: rotated,
                           13: rotated_back, 16: attended, 18: conv_turned, 26: x1_turned}
                for n in range(H * EC):
                    h, c = divmod(n, EC)
                    pe.wait_ge(z_ready, upto(z_ready, n + 1))
                    if not last_batch and n == 0:
                        upto.ahead = 1
                        pe.wait_ge(hT_ready, upto(hT_ready, 1))
                        upto.ahead = 0
                    for i in range(2):
                        last = mm(bank(i), o_w[:, n, :], z[:, n % 4, i * 512:(i + 1) * 512],
                                  start=n == 0, stop=n == H * EC - 1)
                    last.then_inc(z_used, 1)
                    if c == 2 and h % 2 == 0 and h + 2 < H:
                        turn_pair(h + 2)
                    if c == 1 and h + 1 < H:
                        spread_experts(h + 1)
                    if n == 0:
                        pe.wait_ge(o_ready, upto(o_ready, 2 * H))
                    if not last_batch and n in between:
                        upto.ahead = 1
                        between[n]()
                        upto.ahead = 0
                if not last_batch:
                    upto.ahead = 1
                    pe.wait_ge(h2_lo_ready, upto(h2_lo_ready, 1))
                    projection(0)
                    upto.ahead = 0
                pe.wait_ge(yT_ready, upto(yT_ready, 1))
                transpose_tiles(2, lambda t: yT[:, t * 128:(t + 1) * 128], y_ps)
                if not last_batch:
                    upto.ahead = 1
                    projection(1)
                    upto.ahead = 0
                upto.next_batch()

            for step in (x_turned, h_turned, keys, queries, keys_values, rotated, rotated_back, attended, conv_turned,
                         x1_turned):
                step()
            pe.wait_ge(w_lo_ready, 2)
            pe.wait_ge(h2_lo_ready, upto(h2_lo_ready, 1))
            projection(0)
            projection(1)
            upto.enter_loop()
            with pe.Fori(0, B - 1):
                batch(False)
            batch(True)


def constants():
    p = np.arange(128)
    theta = (np.float32(1.0) / np.float32(10000.0) ** (np.arange(C // 2, dtype=np.float32) / np.float32(C // 2)))
    cos, sin = np.cos(theta.astype(np.float32)), np.sin(theta.astype(np.float32))
    rot = np.zeros((C, C), np.float32)
    even = 2 * np.arange(C // 2)
    rot[even, even], rot[even, even + 1], rot[even + 1, even], rot[even + 1, even + 1] = cos, -sin, sin, cos
    parts = {
        "ident": np.eye(128),
        "rot": rot, "rot_t": rot.T,
        "same_head": (p[:, None] // LD == p[None, :] // LD) / N,
        "head_of": (p[:, None] // LD == np.arange(LH)[None, :]) / N,
        "rank": np.broadcast_to(E - np.arange(E), (128, E)),
        "expert_of": 2 * np.arange(EC)[None, :] + p[:, None] // K,
        "causal": np.where(p[None, :] > p[:, None], MASKED, 0.0),
        "causal_t": np.where(p[:, None] > p[None, :], MASKED, 0.0),
        "row_of": (p[:, None] == np.arange(H * 128)[None, :] // 128),
    }
    return np.concatenate([np.asarray(parts[n], np.float32) for n in CONSTS], axis=1)


def kernel(L0_attn_x, L0_attn_W_qk, L0_attn_b_qk, L0_attn_lepe_w, L0_attn_lepe_b, L0_ffn_w_q, L0_ffn_w_k,
           L0_ffn_w_gate, L0_ffn_value_experts, L0_ffn_output_experts, L0_c, L0_wmod):
    import concourse.bacc as bacc
    from concourse.bass_utils import run_bass_kernel_spmd

    b_qk = np.asarray(L0_attn_b_qk)
    arrays = dict(
        x=L0_attn_x,
        w_qk_t=np.asarray(L0_attn_W_qk).T,
        b_q=b_qk[:C].reshape(C, 1), b_k=b_qk[C:].reshape(1, C),
        lepe_w=np.asarray(L0_attn_lepe_w).reshape(C, 3), lepe_b=np.asarray(L0_attn_lepe_b).reshape(C, 1),
        w_q=L0_ffn_w_q, w_k=L0_ffn_w_k, w_gate=L0_ffn_w_gate,
        v_exp=np.asarray(L0_ffn_value_experts).transpose(2, 0, 1, 3).reshape(C, E, H * K),
        o_exp=np.asarray(L0_ffn_output_experts).reshape(EC, 2, H, K, C).transpose(1, 3, 2, 0, 4).reshape(
            128, H * EC, C),
        c_t=np.asarray(L0_c).T, w_mod=L0_wmod, consts=constants(),
    )
    arrays = {n: np.ascontiguousarray(a) for n, a in arrays.items()}
    nc = bacc.Bacc("TRN2", target_bir_lowering=False, num_devices=1)
    aps = {n: nc.dram_tensor(n, a.shape, mybir.dt.from_np(a.dtype), kind="ExternalInput").ap()
           for n, a in arrays.items()}
    out = nc.dram_tensor("out", (B, N, C), mybir.dt.float32, kind="ExternalOutput").ap()
    adaln_block(nc, out=out, **aps)
    return run_bass_kernel_spmd(nc, [arrays], core_ids=[0]).results[0]["out"]
```
